# Optimizing a Trainium2 kernel written in Bass

```python
import numpy as np
import jax
import jax.numpy as jnp

def _softmax(x, axis=-1):
    return jax.nn.softmax(x, axis=axis)

def _gelu(x):
    return jax.nn.gelu(x, approximate=True)

def _silu(x):
    return jax.nn.silu(x)

def _sigmoid(x):
    return jax.nn.sigmoid(x)

def _layernorm(x, axis=-1, eps=1e-05):
    m = jnp.mean(x, axis=axis, keepdims=True)
    v = jnp.var(x, axis=axis, keepdims=True)
    return (x - m) / jnp.sqrt(v + eps)

def _scatter_add(tgt, idx, src, axis=0):
    return tgt.at[idx].add(src)

def _segment_sum(src, seg, n):
    return jax.ops.segment_sum(src, seg, n)
kernel_name = 'mk_seq_preln_d1_jaxref_r8_de9815'

def setup_inputs(seed: int=0):
    np.random.seed(seed)
    _w = jnp.asarray

    def _L0_attn_setup():
        import jax, jax.numpy as jnp
        import numpy as np
        N_HEAD = 16
        GAMMA_MIN = 0.9
        GAMMA_MAX = 0.999
        GN_EPS = 1e-05

        def _gammas(n_head):
            lo = float(np.log(1.0 - GAMMA_MAX))
            hi = float(np.log(1.0 - GAMMA_MIN))
            return 1.0 - jnp.exp(jnp.linspace(lo, hi, n_head, dtype=jnp.float32))
        key = jax.random.key(seed)
        ks = jax.random.split(key, 5)
        B, T, C = (2, 256, 128)
        scale = 0.02
        return {'x': jax.random.normal(ks[0], (B, T, C), dtype=jnp.float32), 'wq': jax.random.normal(ks[1], (C, C), dtype=jnp.float32) * scale, 'wk': jax.random.normal(ks[2], (C, C), dtype=jnp.float32) * scale, 'wv': jax.random.normal(ks[3], (C, C), dtype=jnp.float32) * scale, 'wo': jax.random.normal(ks[4], (C, C), dtype=jnp.float32) * scale, 'gn_w': jnp.ones((C,), dtype=jnp.float32), 'gn_b': jnp.zeros((C,), dtype=jnp.float32)}
    _L0_attn_in = _L0_attn_setup()

    def _L0_ffn_setup():
        import jax, jax.numpy as jnp
        import numpy as np
        D = 128
        F = 128
        E = 8
        K = 2
        B, T = (2, 256)

        def _moe_forward(x, router_w, w1, w2, shared_gate_up, shared_down, shared_gate_w):
            b, t, d = x.shape
            xf = x.reshape(-1, d)
            n = xf.shape[0]
            logits = xf @ router_w
            probs = jax.nn.softmax(logits, axis=-1)
            topw, topi = jax.lax.top_k(probs, K)
            combine = jnp.zeros((n, E), dtype=probs.dtype).at[jnp.arange(n)[:, None], topi].add(topw)
            h = jax.nn.silu(jnp.einsum('nd,edf->nef', xf, w1))
            ye = jnp.einsum('nef,efd->ned', h, w2)
            routed = jnp.einsum('ne,ned->nd', combine, ye)
            gu = xf @ shared_gate_up
            gate, up = (gu[:, :F], gu[:, F:])
            shared = jax.nn.silu(gate) * up @ shared_down
            shared = jax.nn.sigmoid(xf @ shared_gate_w) * shared
            return (routed + shared).reshape(b, t, d)
        key = jax.random.key(seed)
        ks = jax.random.split(key, 7)
        std = 0.02
        x = jax.random.normal(ks[0], (B, T, D), dtype=jnp.float32)
        router_w = jax.random.normal(ks[1], (D, E), dtype=jnp.float32) * std
        w1 = jax.random.normal(ks[2], (E, D, F), dtype=jnp.float32) * std
        w2 = jax.random.normal(ks[3], (E, F, D), dtype=jnp.float32) * std
        shared_gate_up = jax.random.normal(ks[4], (D, 2 * F), dtype=jnp.float32) * std
        shared_down = jax.random.normal(ks[5], (F, D), dtype=jnp.float32) * std
        shared_gate_w = jax.random.normal(ks[6], (D, 1), dtype=jnp.float32) * std
        return {'x': x, 'router_w': router_w, 'w1': w1, 'w2': w2, 'shared_gate_up': shared_gate_up, 'shared_down': shared_down, 'shared_gate_w': shared_gate_w}
    _L0_ffn_in = _L0_ffn_setup()
    _d = {'L0_attn_x': _L0_attn_in['x'], 'L0_attn_wq': _L0_attn_in['wq'], 'L0_attn_wk': _L0_attn_in['wk'], 'L0_attn_wv': _L0_attn_in['wv'], 'L0_attn_wo': _L0_attn_in['wo'], 'L0_attn_gn_w': _L0_attn_in['gn_w'], 'L0_attn_gn_b': _L0_attn_in['gn_b'], 'L0_ffn_router_w': _L0_ffn_in['router_w'], 'L0_ffn_w1': _L0_ffn_in['w1'], 'L0_ffn_w2': _L0_ffn_in['w2'], 'L0_ffn_shared_gate_up': _L0_ffn_in['shared_gate_up'], 'L0_ffn_shared_down': _L0_ffn_in['shared_down'], 'L0_ffn_shared_gate_w': _L0_ffn_in['shared_gate_w']}
    _x0 = _d['L0_attn_x']
    _d['L0_attn_x'] = jax.random.normal(jax.random.fold_in(jax.random.key(seed), 1), (16, 512, 128), dtype=_x0.dtype)
    del _x0
    return _d

def reference(L0_attn_x, L0_attn_wq, L0_attn_wk, L0_attn_wv, L0_attn_wo, L0_attn_gn_w, L0_attn_gn_b, L0_ffn_router_w, L0_ffn_w1, L0_ffn_w2, L0_ffn_shared_gate_up, L0_ffn_shared_down, L0_ffn_shared_gate_w):

    def _L0_attn_ref(x, wq, wk, wv, wo, gn_w, gn_b):
        import jax, jax.numpy as jnp
        import numpy as np
        N_HEAD = 16
        GAMMA_MIN = 0.9
        GAMMA_MAX = 0.999
        GN_EPS = 1e-05

        def _gammas(n_head):
            lo = float(np.log(1.0 - GAMMA_MAX))
            hi = float(np.log(1.0 - GAMMA_MIN))
            return 1.0 - jnp.exp(jnp.linspace(lo, hi, n_head, dtype=jnp.float32))
        B, T, C = x.shape
        H = N_HEAD
        d = C // H
        gammas = _gammas(H)
        q = (x @ wq.T).reshape(B, T, H, d).transpose(0, 2, 1, 3)
        k = (x @ wk.T).reshape(B, T, H, d).transpose(0, 2, 1, 3)
        v = (x @ wv.T).reshape(B, T, H, d).transpose(0, 2, 1, 3)
        pos = jnp.arange(T, dtype=jnp.float32)
        dist = pos[:, None] - pos[None, :]
        causal = dist >= 0
        safe_dist = jnp.where(causal, dist, 0.0)
        D = jnp.where(causal, gammas[:, None, None] ** safe_dist, 0.0)
        scores = jnp.einsum('bhid,bhjd->bhij', q, k) * D
        y = jnp.einsum('bhij,bhjd->bhid', scores, v)
        y = y.transpose(0, 2, 1, 3)
        mean = y.mean(axis=(1, 3), keepdims=True)
        var = y.var(axis=(1, 3), keepdims=True)
        y = (y - mean) * jax.lax.rsqrt(var + GN_EPS)
        y = y.reshape(B, T, C) * gn_w + gn_b
        return y @ wo.T

    def _L0_ffn_ref(x, router_w, w1, w2, shared_gate_up, shared_down, shared_gate_w):
        import jax, jax.numpy as jnp
        import numpy as np
        D = 128
        F = 128
        E = 8
        K = 2
        B, T = (2, 256)

        def _moe_forward(x, router_w, w1, w2, shared_gate_up, shared_down, shared_gate_w):
            b, t, d = x.shape
            xf = x.reshape(-1, d)
            n = xf.shape[0]
            logits = xf @ router_w
            probs = jax.nn.softmax(logits, axis=-1)
            topw, topi = jax.lax.top_k(probs, K)
            combine = jnp.zeros((n, E), dtype=probs.dtype).at[jnp.arange(n)[:, None], topi].add(topw)
            h = jax.nn.silu(jnp.einsum('nd,edf->nef', xf, w1))
            ye = jnp.einsum('nef,efd->ned', h, w2)
            routed = jnp.einsum('ne,ned->nd', combine, ye)
            gu = xf @ shared_gate_up
            gate, up = (gu[:, :F], gu[:, F:])
            shared = jax.nn.silu(gate) * up @ shared_down
            shared = jax.nn.sigmoid(xf @ shared_gate_w) * shared
            return (routed + shared).reshape(b, t, d)
        return _moe_forward(x, router_w, w1, w2, shared_gate_up, shared_down, shared_gate_w)
    x = L0_attn_x
    x = x + _L0_attn_ref(_layernorm(x, axis=-1), L0_attn_wq, L0_attn_wk, L0_attn_wv, L0_attn_wo, L0_attn_gn_w, L0_attn_gn_b)
    x = x + _L0_ffn_ref(_layernorm(x, axis=-1), L0_ffn_router_w, L0_ffn_w1, L0_ffn_w2, L0_ffn_shared_gate_up, L0_ffn_shared_down, L0_ffn_shared_gate_w)
    return x

_drawn_inputs = setup_inputs


def setup_inputs(seed=0):
    import zlib

    import numpy as np

    out = dict(_drawn_inputs(seed))
    spreads = {'L0_attn_gn_w': (1.0, 0.2), 'L0_attn_gn_b': (0.0, 0.379)}
    factors = {'L0_ffn_router_w': 8.0,
     'L0_ffn_w1': 8.0,
     'L0_ffn_w2': 8.0,
     'L0_ffn_shared_gate_up': 8.0,
     'L0_ffn_shared_down': 8.0,
     'L0_ffn_shared_gate_w': 8.0}
    for name, (base, spread) in spreads.items():
        noise = np.random.default_rng([zlib.crc32(name.encode()), seed]).standard_normal(out[name].shape)
        drawn = base * np.exp(spread * noise) if base else spread * noise
        out[name] = jnp.asarray(drawn.astype(out[name].dtype))
    for name, factor in factors.items():
        out[name] = (out[name] * factor).astype(out[name].dtype)
    return out
```

```python
import concourse.bass as bass
from concourse import mybir
from contextlib import ExitStack

B, T, C = 16, 512, 128
H, HD = 16, 8
E = 8
P = 128
NT = T // P
HQ = 4
NQ = H // HQ
HALF = C // 2
EPS = 1e-5

RA = 3
A_XT, A_HALF, A_QT, A_SELQ, A_KV, A_SELK, A_TILE = 0, 1, 5, 6, 10, 14, 18
A_USES = A_TILE + 5 * NT - 1
RF = 2
F_GN, F_OUT, F_XT, F_LG, F_GATE, F_UP, F_EXP, F_USES = 0, 1, 2, 3, 4, 5, 6, 14
RM = 2
M_USES = 3 * NT
GROUPS = [(0, 1, 2, 3), (4, 5, 6, 7), (8,)]
DQ = 3
SILU = 9
MOE = 9
ROUTE = 13


def a_s(t, q):
    return A_TILE + 5 * t + q


def a_u(t):
    return A_TILE + 5 * t + 4


def later(b):
    return not isinstance(b, int) or b > 0


def preln_layer_kernel(nc, x_d, wqkv_d, wo_d, w1_d, w2_d, rw_d, gn_d, decay_d, mats_d, out_d):
    f32 = mybir.dt.float32
    f32r = mybir.dt.float32r
    ALU = mybir.AluOpType
    ACT = mybir.ActivationFunctionType
    AX = mybir.AxisListType

    x_v = x_d.rearrange("b (t p) c -> b p t c", p=P)
    out_v = out_d.rearrange("b (t p) c -> b p t c", p=P)

    ctx = ExitStack()
    with ctx:
        def sb(name, shape, dt=f32):
            return ctx.enter_context(nc.sbuf_tensor(name, shape, dt))

        def sem(name):
            return ctx.enter_context(nc.semaphore(name))

        decay = sb("decay", [P, H, P])
        mats = sb("mats", [P, 10, P])
        ident, g_up, g_down, bdmask, avg8 = (mats[:, n, :] for n in range(5))
        gC, iota = mats[:, 9, 0:1], mats[:, 9, 8:8 + E]
        sel = sb("sel", [P, 4, P], f32r)
        gnp = sb("gnp", [P, 2])
        wqkv = sb("wqkv", [P, 3 * C])
        wo = sb("wo", [P, C])
        w1 = sb("w1", [P, 10 * C])
        w2 = sb("w2", [P, 9 * C])
        rw = sb("rw", [P, 9])
        wh_hi = sb("wh_hi", [P, 4, 2, HALF], f32r)
        wh_lo = sb("wh_lo", [P, 4, 2, HALF], f32r)
        wqkv_hi = sb("wqkv_hi", [P, 3 * C], f32r)
        wqkv_lo = sb("wqkv_lo", [P, 3 * C], f32r)
        w1_hi = sb("w1_hi", [P, 10 * C], f32r)
        w1_lo = sb("w1_lo", [P, 10 * C], f32r)
        rw_s = sb("rw_s", [P, 2 * C], f32r)
        xin = sb("xin", [P, 2, NT, C])
        xn = sb("xn", [P, NT, C])
        xT_hi = sb("xT_hi", [P, T], f32r)
        xT_lo = sb("xT_lo", [P, T], f32r)
        halves = sb("halves", [P, 4, T], f32r)
        qt = sb("qt", [P, T])
        q4 = sb("q4", [P, NQ, T], f32r)
        k4 = sb("k4", [P, NQ, T], f32r)
        qbd = sb("qbd", [P, NQ, NT, HQ, P], f32r)
        kt = sb("kt", [P, NT, C])
        vbd = sb("vbd", [P, NT, HQ, C])
        sm = sb("sm", [P, 2, NQ, HQ * P])
        s_raw = sb("s_raw", [P, 2, HQ * P])
        state = sb("state", [P, C])
        state_m = sb("state_m", [P, NT - 1, C])
        yn = sb("yn", [P, T])
        st1 = sb("st1", [P, NT, 6])
        mv1 = sb("mv1", [P, NT, 2])
        ve1 = sb("ve1", [P, NT])
        rs1 = sb("rs1", [P, NT])
        gst = sb("gst", [P, 6])
        gmv = sb("gmv", [P, 2])
        gm = sb("gm", [P, 2])
        gvar = sb("gvar", [P, 1])
        gve = sb("gve", [P, 1])
        grs = sb("grs", [P, 1])
        gab = sb("gab", [P, 2])
        mhalf = sb("mhalf", [P, NT])
        res = sb("res", [P, 2, NT, C])
        st2 = sb("st2", [P, NT, 6])
        mv2 = sb("mv2", [P, NT, 2])
        ve2 = sb("ve2", [P, NT])
        rs2 = sb("rs2", [P, NT])
        x2n = sb("x2n", [P, NT, C])
        x2T_hi = sb("x2T_hi", [P, T], f32r)
        x2T_lo = sb("x2T_lo", [P, T], f32r)
        lgc = sb("lgc", [P, NT, 18])
        lg = sb("lg", [P, NT, 9])
        mx = sb("mx", [P, NT, 8])
        ix = sb("ix", [P, NT, 8], mybir.dt.uint32)
        dd = sb("dd", [P, NT, 9])
        ee = sb("ee", [P, NT, 9])
        m0 = sb("m0", [P, NT, 8])
        m1 = sb("m1", [P, NT, 8])
        den = sb("den", [P, NT, 2])
        rden = sb("rden", [P, NT, 2])
        em = sb("em", [P, NT, 8])
        cw = sb("cw", [P, NT, 9])
        gate = sb("gate", [P, T])
        hh = sb("hh", [P, 9, T])
        carrier = sb("carrier", [P, 1])
        accb = sb("accb", [P, 2, C])

        bankA = [ctx.enter_context(nc.psum_tensor(f"bankA{i}", [P, 512], f32)) for i in range(RA)]
        bankY = ctx.enter_context(nc.psum_tensor("bankY", [P, T], f32))
        bankF = [ctx.enter_context(nc.psum_tensor(f"bankF{i}", [P, 512], f32)) for i in range(RF)]
        bankM = [ctx.enter_context(nc.psum_tensor(f"bankM{i}", [P, 512], f32)) for i in range(RM)]

        def A(u):
            return bankA[u % RA]

        def F(u):
            return bankF[u % RF]

        def M(u):
            return bankM[u % RM]

        def diag(t):
            v = vbd[:, t, 0, :]
            return bass.AP(v.tensor, v.offset, [list(v.ap[0]), [HQ * HD, NQ], [C + HD, HQ], [1, HD]])

        def per(v, n):
            return bass.AP(v.tensor, v.offset, [list(p) for p in v.ap] + [[0, n]])

        def rep(v, n):
            return bass.AP(v.tensor, v.offset, [list(v.ap[0]), [0, n]] + [list(p) for p in v.ap[1:]])

        w_loaded = sem("w_loaded")
        x_loaded = sem("x_loaded")
        q_spread = sem("q_spread")
        out_stored = sem("out_stored")
        setup_pool = sem("setup_pool")
        setup_hi = sem("setup_hi")
        setup_dve = sem("setup_dve")
        ln1_rstd = sem("ln1_rstd")
        ln2_rstd = sem("ln2_rstd")
        gn_rstd = sem("gn_rstd")
        pool_s = sem("pool_s")
        a_full = sem("a_full")
        f_full = sem("f_full")
        m_full = sem("m_full")
        y_full = sem("y_full")
        act_xhi = sem("act_xhi")
        act_half = sem("act_half")
        act_q4 = sem("act_q4")
        act_k4 = sem("act_k4")
        act_v = sem("act_v")
        act_s = sem("act_s")
        act_yn = sem("act_yn")
        act_x2hi = sem("act_x2hi")
        act_lg = sem("act_lg")
        act_exp = sem("act_exp")
        act_silu = sem("act_silu")
        ln1_step = sem("ln1_step")
        ln1_var = sem("ln1_var")
        xn_ready = sem("xn_ready")
        dve_xlo = sem("dve_xlo")
        dve_half = sem("dve_half")
        dve_qt = sem("dve_qt")
        dve_kt = sem("dve_kt")
        dve_s = sem("dve_s")
        dve_state = sem("dve_state")
        dve_statem = sem("dve_statem")
        gn_step = sem("gn_step")
        gn_stats = sem("gn_stats")
        gn_mean = sem("gn_mean")
        gn_diff = sem("gn_diff")
        gn_var = sem("gn_var")
        gn_scale = sem("gn_scale")
        gn_ab = sem("gn_ab")
        dve_x1 = sem("dve_x1")
        ln2_step = sem("ln2_step")
        ln2_var = sem("ln2_var")
        x2n_ready = sem("x2n_ready")
        dve_x2lo = sem("dve_x2lo")
        dve_route = sem("dve_route")
        dve_up = sem("dve_up")
        dve_moe = sem("dve_moe")
        dve_out = sem("dve_out")

        A_FREED = [(dve_xlo, 1, 1)] + [(dve_half, 4, n + 1) for n in range(4)] + [(dve_qt, 1, 1)]
        A_FREED += [(act_q4, NQ, n + 1) for n in range(NQ)]
        A_FREED += [(dve_kt, NT, t + 1) for t in range(NT)]
        A_FREED += [(act_k4, NQ, n + 1) for n in range(NQ)]
        for t in range(NT):
            A_FREED += [(dve_s, DQ * NT, DQ * t + q + 1) for q in range(DQ)] + [(act_s, NT, t + 1)]
            A_FREED += [(dve_state, NT - 1, t + 1)] if t < NT - 1 else []
        F_FREED = [(gn_mean, 1, 1), (dve_x1, 1, 1), (dve_x2lo, 1, 1), (act_lg, 1, 1), (act_silu, SILU, 1),
                   (dve_up, 1, 1)] + [(act_silu, SILU, 2 + e) for e in range(E)]
        M_FREED = [(dve_moe, MOE * NT, MOE * t + g) for t in range(NT) for g in (4, 8, 9)]
        assert len(A_FREED) == A_USES and len(F_FREED) == F_USES and len(M_FREED) == M_USES

        def freed(table, ring, b, u):
            s, per_seq, k = table[u - ring]
            return s, (b if u >= ring else b - 1) * per_seq + k

        def sequence(dram, b):
            return dram[b] if isinstance(b, int) else dram[bass.ds(b, 1)].rearrange("o p t c -> (o p) t c")

        block = ctx.enter_context(nc.Block())

        def iterations(eng, steps):
            steps(0, 0, True, False, False, True)
            steps(1, 1, True, True, False, True)
            steps(2, 0, True, True, True, True)
            with eng.Fori(0, (B - 4) // 2) as k:
                steps(2 * k + 3, 1, True, True, True, True)
                steps(2 * k + 4, 0, True, True, True, True)
            steps(B - 1, 1, True, True, True, False)
            steps(B, 0, False, True, True, False)
            steps(B + 1, 1, False, False, True, False)

        @block.sync
        def _(sp):
            sp.dma_start(xin[:, 0], x_v[0]).then_inc(x_loaded, 16)
            for dst, src in ((wqkv[:], wqkv_d), (mats[:], mats_d), (w1[:], w1_d), (rw[:], rw_d), (gnp[:], gn_d),
                             (wo[:], wo_d), (decay[:], decay_d), (w2[:], w2_d)):
                sp.dma_start(dst, src).then_inc(w_loaded, 16)
            sp.wait_ge(setup_pool, 2)

            def steps(b, p, att, ffn, moe, nxt):
                if nxt:
                    if later(b):
                        sp.wait_ge(dve_x1, b)
                    else:
                        sp.wait_ge(ln1_step, 1)
                    sp.dma_start(xin[:, 1 - p], sequence(x_v, b + 1)).then_inc(x_loaded, 16)
                if att:
                    sp.wait_ge(act_q4, b * NQ + NQ)
                    if later(b):
                        sp.wait_ge(a_full, (b - 1) * A_USES + A_USES)
                    for h in range(HQ):
                        rows = slice(32 * h, 32 * h + 32)
                        sp.dma_start(qbd[rows, :, :, h, :].bitcast(f32),
                                     q4[rows, :, :].rearrange("p q (t i) -> p q t i", t=NT).bitcast(f32)
                                     ).then_inc(q_spread, 16)
                if moe:
                    sp.wait_ge(dve_out, (b - 2) * NT + NT)
                    sp.dma_start(sequence(out_v, b - 2), res[:, p]).then_inc(out_stored, 16)

            iterations(sp, steps)
            sp.wait_ge(out_stored, 16 * B)

        @block.gpsimd
        def _(pool):
            nc.gpsimd.memset(mhalf[:], -0.5).then_inc(setup_pool, 1)
            nc.gpsimd.memset(qbd[:].bitcast(f32), 0.0).then_inc(setup_pool, 1)
            nc.gpsimd.memset(vbd[:], 0.0).then_inc(setup_pool, 1)
            pool.wait_ge(setup_pool, 1)
            pool.wait_ge(ln1_var, 1)
            nc.gpsimd.tensor_tensor(rs1[:], ve1[:], mhalf[:], ALU.pow).then_inc(ln1_rstd, 1)
            pool.wait_ge(w_loaded, 16 * 8)

            def steps(b, p, att, ffn, moe, nxt):
                f = b - 1

                def scores(t):
                    if att:
                        pool.wait_ge(act_s, b * NT + t + 1)
                        nc.gpsimd.tensor_tensor(sm[:, t % 2, DQ, :], s_raw[:, t % 2, :],
                                                decay[:, HQ * DQ:, :].rearrange("p h i -> p (h i)"),
                                                ALU.mult).then_inc(pool_s, 1)

                if ffn:
                    pool.wait_ge(gn_var, f + 1)
                    nc.gpsimd.tensor_tensor(grs[:], gve[:], mhalf[:, 0:1], ALU.pow).then_inc(gn_rstd, 1)
                    pool.wait_ge(ln2_var, f + 1)
                    nc.gpsimd.tensor_tensor(rs2[:], ve2[:], mhalf[:], ALU.pow).then_inc(ln2_rstd, 1)
                scores(0)
                scores(1)
                scores(2)
                if nxt:
                    pool.wait_ge(ln1_var, b + 2)
                    nc.gpsimd.tensor_tensor(rs1[:], ve1[:], mhalf[:], ALU.pow).then_inc(ln1_rstd, 1)
                scores(3)

            iterations(pool, steps)

        @block.scalar
        def _(act):
            def copy(out, in_):
                return nc.scalar.activation(out, in_, ACT.Copy)

            def steps(b, p, att, ffn, moe, nxt):
                f = b - 1

                def half(n):
                    if att:
                        act.wait_ge(a_full, b * A_USES + A_HALF + n + 1)
                        copy(halves[:, n, :], A(A_HALF + n)[:, :]).then_inc(act_half, 1)

                def q_terms(n):
                    if att:
                        act.wait_ge(a_full, b * A_USES + A_SELQ + n + 1)
                        if n == 0 and later(b):
                            act.wait_ge(q_spread, (b - 1) * 16 * HQ + 16 * HQ)
                        copy(q4[:, n, :], A(A_SELQ + n)[:, :]).then_inc(act_q4, 1)

                def k_terms(n):
                    if att:
                        act.wait_ge(a_full, b * A_USES + A_SELK + n + 1)
                        copy(k4[:, n, :], A(A_SELK + n)[:, :]).then_inc(act_k4, 1)

                def values(t):
                    if att:
                        act.wait_ge(a_full, b * A_USES + A_KV + t + 1)
                        copy(diag(t), A(A_KV + t)[:, C:2 * C].rearrange("p (q h c) -> p q h c", q=NQ, h=HQ)
                             ).then_inc(act_v, 1)

                def scores(t):
                    if att:
                        act.wait_ge(a_full, b * A_USES + a_s(t, DQ) + 1)
                        if t >= 2 or later(b):
                            act.wait_ge(pool_s, b * NT + t - 1)
                        copy(s_raw[:, t % 2, :], A(a_s(t, DQ))[:, :]).then_inc(act_s, 1)

                def silu(e):
                    if ffn:
                        act.wait_ge(f_full, f * F_USES + F_EXP + e + 1)
                        nc.scalar.activation(hh[:, e, :], F(F_EXP + e)[:, :], ACT.Silu).then_inc(act_silu, 1)

                if att:
                    act.wait_ge(a_full, b * A_USES + A_XT + 1)
                    copy(xT_hi[:], A(A_XT)[:, :]).then_inc(act_xhi, 1)
                half(0)
                half(1)
                half(2)
                half(3)
                if ffn:
                    act.wait_ge(gn_ab, f + 1)
                    nc.scalar.activation(yn[:], bankY[:, :], ACT.Identity, scale=gab[:, 0:1],
                                         bias=gab[:, 1:2]).then_inc(act_yn, 1)
                for n in range(NQ):
                    q_terms(n)
                for t in range(NT):
                    values(t)
                for n in range(NQ):
                    k_terms(n)
                if ffn:
                    act.wait_ge(f_full, f * F_USES + F_XT + 1)
                    copy(x2T_hi[:], F(F_XT)[:, :]).then_inc(act_x2hi, 1)
                    act.wait_ge(f_full, f * F_USES + F_LG + 1)
                    if later(f):
                        act.wait_ge(dve_route, (f - 1) * ROUTE + 1)
                    copy(lgc[:], F(F_LG)[:, 0:32 * NT].rearrange("p (t c) -> p t c", t=NT)[:, :, 0:18]
                         ).then_inc(act_lg, 1)
                scores(0)
                if ffn:
                    act.wait_ge(dve_route, f * ROUTE + 3)
                    nc.scalar.activation(ee[:], dd[:], ACT.Exp).then_inc(act_exp, 1)
                    act.wait_ge(f_full, f * F_USES + F_GATE + 1)
                    if later(f):
                        act.wait_ge(dve_up, f)
                    nc.scalar.activation(gate[:], F(F_GATE)[:, :], ACT.Silu).then_inc(act_silu, 1)
                silu(0)
                silu(1)
                scores(1)
                silu(2)
                silu(3)
                silu(4)
                scores(2)
                silu(5)
                silu(6)
                scores(3)
                silu(7)

            act.wait_ge(setup_pool, 3)
            iterations(act, steps)

        @block.vector
        def _(dve):
            def low(dst, full, hi, ready):
                nc.vector.tensor_tensor(dst, full, hi.bitcast(f32), ALU.subtract).then_inc(ready, 1)

            def stats1(src, st, step):
                for t in range(NT):
                    last = nc.vector.bn_stats(st[:, t, :], src[:, t, :])
                last.then_inc(step, 1)

            def stats2(b, st, mv, step):
                dve.wait_ge(step, 2 * b + 1)
                nc.vector.memset(carrier[:], 0.0)
                for t in range(NT):
                    last = nc.vector.bn_aggr(mv[:, t, :], st[:, t, :])
                last.then_inc(step, 1)

            def stats3(b, mv, ve, step, var):
                dve.wait_ge(step, 2 * b + 2)
                nc.vector.tensor_scalar(ve[:], mv[:, :, 1], EPS, None, ALU.add).then_inc(var, 1)

            def normalise(b, dst, src, mv, rs, rstd, ready):
                dve.wait_ge(rstd, b + 1)
                for t in range(NT):
                    last = nc.vector.tensor_scalar(dst[:, t, :], src[:, t, :], mv[:, t, 0:1], rs[:, t:t + 1],
                                                   ALU.subtract, ALU.mult)
                last.then_inc(ready, 1)

            def steps(b, p, att, ffn, moe, nxt):
                f, m, pf = b - 1, b - 2, 1 - p

                def half(n):
                    if att:
                        dve.wait_ge(act_half, b * 4 + n + 1)
                        low(halves[HALF:, n, :], A(A_HALF + n)[HALF:, :], halves[HALF:, n, :], dve_half)

                def k_decay(t):
                    if att:
                        dve.wait_ge(act_v, b * NT + t + 1)
                        nc.vector.tensor_tensor(kt[:, t, :], A(A_KV + t)[:, 0:C], g_down,
                                                ALU.mult).then_inc(dve_kt, 1)

                def scores(t, q):
                    if att:
                        dve.wait_ge(a_full, b * A_USES + a_s(t, q) + 1)
                        nc.vector.tensor_tensor(sm[:, t % 2, q, :].rearrange("p (h i) -> p h i", h=HQ),
                                                A(a_s(t, q))[:, :].rearrange("p (h i) -> p h i", h=HQ),
                                                decay[:, HQ * q:HQ * q + HQ, :], ALU.mult).then_inc(dve_s, 1)

                def state_add(t):
                    if att:
                        dve.wait_ge(a_full, b * A_USES + a_u(t) + 1)
                        if t == 0:
                            nc.vector.tensor_copy(state[:], A(a_u(t))[:, 0:C]).then_inc(dve_state, 1)
                        else:
                            nc.vector.scalar_tensor_tensor(state[:], state[:], gC, A(a_u(t))[:, 0:C],
                                                           ALU.mult, ALU.add).then_inc(dve_state, 1)

                def state_mask(t):
                    if att:
                        dve.wait_ge(dve_state, b * (NT - 1) + t + 1)
                        nc.vector.tensor_tensor(state_m[:, t, :], state[:], bdmask, ALU.mult).then_inc(dve_statem, 1)

                def combine(t, g):
                    if not moe:
                        return
                    bank = M(3 * t + g)
                    dve.wait_ge(m_full, m * M_USES + 3 * t + g + 1)
                    for e in GROUPS[g]:
                        y, w = bank[:, (e % 4) * C:(e % 4) * C + C], cw[:, t, e:e + 1]
                        acc = accb[:, t % 2, :] if e % 2 else res[:, p, t, :]
                        if e >= 2:
                            dve.wait_ge(dve_moe, m * MOE * NT + MOE * t + e - 1)
                        if e == 1:
                            nc.vector.tensor_scalar(acc, y, w, None, ALU.mult).then_inc(dve_moe, 1)
                        else:
                            nc.vector.scalar_tensor_tensor(acc, y, w, acc, ALU.mult, ALU.add).then_inc(dve_moe, 1)

                def total(t):
                    if moe:
                        dve.wait_ge(dve_moe, m * MOE * NT + MOE * t + MOE)
                        nc.vector.tensor_tensor(res[:, p, t, :], res[:, p, t, :], accb[:, t % 2, :],
                                                ALU.add).then_inc(dve_out, 1)

                def gn_sums():
                    if ffn:
                        dve.wait_ge(y_full, f * NT + NT)
                        nc.vector.bn_stats(gst[:], bankY[:, :]).then_inc(gn_step, 1)
                        dve.wait_ge(gn_step, 2 * f + 1)
                        nc.vector.memset(carrier[:], 0.0)
                        nc.vector.bn_aggr(gmv[:], gst[:]).then_inc(gn_step, 1)

                def gn_square():
                    if ffn:
                        dve.wait_ge(gn_step, 2 * f + 2)
                        nc.vector.scalar_tensor_tensor(gmv[:, 1:2], gmv[:, 0:1], gmv[:, 0:1], gmv[:, 1:2],
                                                       ALU.mult, ALU.add).then_inc(gn_stats, 1)

                def gn_variance():
                    if ffn:
                        dve.wait_ge(f_full, f * F_USES + F_GN + 1)
                        nc.vector.tensor_copy(gm[:], F(F_GN)[:, 0:2]).then_inc(gn_mean, 1)
                        dve.wait_ge(gn_mean, f + 1)
                        nc.vector.scalar_tensor_tensor(gvar[:], gm[:, 0:1], gm[:, 0:1], gm[:, 1:2], ALU.mult,
                                                       ALU.subtract, reverse1=True).then_inc(gn_diff, 1)
                        dve.wait_ge(gn_diff, f + 1)
                        nc.vector.tensor_scalar(gve[:], gvar[:], 0.0, EPS, ALU.max, ALU.add).then_inc(gn_var, 1)

                def gn_affine():
                    if ffn:
                        dve.wait_ge(gn_rstd, f + 1)
                        nc.vector.tensor_tensor(gab[:, 0:1], grs[:], gnp[:, 0:1], ALU.mult).then_inc(gn_scale, 1)
                        dve.wait_ge(gn_scale, f + 1)
                        nc.vector.scalar_tensor_tensor(gab[:, 1:2], gm[:, 0:1], gab[:, 0:1], gnp[:, 1:2], ALU.mult,
                                                       ALU.subtract, reverse1=True).then_inc(gn_ab, 1)

                def residual():
                    if ffn:
                        dve.wait_ge(f_full, f * F_USES + F_OUT + 1)
                        if not isinstance(b, int) or f >= 2:
                            dve.wait_ge(out_stored, (f - 2) * 16 + 16)
                        nc.vector.tensor_tensor(res[:, pf], F(F_OUT)[:, :].rearrange("p (t c) -> p t c", t=NT),
                                                xin[:, pf], ALU.add).then_inc(dve_x1, 1)

                def ln2(n):
                    if ffn and n == 0:
                        dve.wait_ge(dve_x1, f + 1)
                        stats1(res[:, pf], st2, ln2_step)
                    elif ffn and n == 1:
                        stats2(f, st2, mv2, ln2_step)
                    elif ffn and n == 2:
                        stats3(f, mv2, ve2, ln2_step, ln2_var)
                    elif ffn:
                        normalise(f, x2n, res[:, pf], mv2, rs2, ln2_rstd, x2n_ready)

                def ln1(n):
                    if nxt and n == 0:
                        dve.wait_ge(x_loaded, (b + 1) * 16 + 16)
                        stats1(xin[:, 1 - p], st1, ln1_step)
                    elif nxt and n == 1:
                        stats2(b + 1, st1, mv1, ln1_step)
                    elif nxt and n == 2:
                        stats3(b + 1, mv1, ve1, ln1_step, ln1_var)
                    elif nxt:
                        normalise(b + 1, xn, xin[:, 1 - p], mv1, rs1, ln1_rstd, xn_ready)

                def route(n):
                    if not ffn:
                        return
                    if n > 0:
                        dve.wait_ge(dve_route, f * ROUTE + n)
                    if n == 0:
                        dve.wait_ge(act_lg, f + 1)
                        ins = nc.vector.tensor_tensor(lg[:], lgc[:, :, 0:9], lgc[:, :, 9:18], ALU.add)
                    elif n == 1:
                        nc.vector.tensor_scalar(dd[:, :, 8], lg[:, :, 8], -1.0, None, ALU.mult)
                        for t in range(NT):
                            ins = nc.vector.max(mx[:, t, :], lg[:, t, 0:E])
                    elif n == 2:
                        ins = nc.vector.tensor_tensor(dd[:, :, 0:E], lg[:, :, 0:E], per(mx[:, :, 0], E),
                                                      ALU.subtract)
                    elif n == 3:
                        nc.vector.memset(carrier[:], 0.0)
                        for t in range(NT):
                            ins = nc.vector.max_index(ix[:, t, :], mx[:, t, :], lg[:, t, 0:E])
                    elif n == 4:
                        ins = nc.vector.tensor_tensor(m0[:], rep(iota, NT), per(ix[:, :, 0], E), ALU.is_equal)
                    elif n == 5:
                        ins = nc.vector.tensor_tensor(m1[:], rep(iota, NT), per(ix[:, :, 1], E), ALU.is_equal)
                    elif n == 6:
                        ins = nc.vector.tensor_tensor(m0[:], m0[:], m1[:], ALU.add)
                    elif n == 7:
                        dve.wait_ge(act_exp, f + 1)
                        ins = nc.vector.tensor_reduce(den[:, :, 0], ee[:, :, 0:E], AX.X, ALU.add)
                    elif n == 8:
                        ins = nc.vector.tensor_scalar(den[:, :, 1], ee[:, :, 8], 1.0, None, ALU.add)
                    elif n == 9:
                        ins = nc.vector.tensor_tensor(em[:], ee[:, :, 0:E], m0[:], ALU.mult)
                    elif n == 10:
                        ins = nc.vector.reciprocal(rden[:], den[:])
                    elif n == 11:
                        ins = nc.vector.tensor_tensor(cw[:, :, 0:E], em[:], per(rden[:, :, 0], E), ALU.mult)
                    else:
                        ins = nc.vector.tensor_copy(cw[:, :, 8], rden[:, :, 1])
                    ins.then_inc(dve_route, 1)

                if att:
                    dve.wait_ge(act_xhi, b + 1)
                    low(xT_lo[:], A(A_XT)[:, :], xT_hi[:], dve_xlo)
                gn_sums()
                half(0)
                gn_square()
                combine(0, 0)
                half(1)
                gn_variance()
                combine(0, 1)
                half(2)
                gn_affine()
                combine(0, 2)
                half(3)
                combine(1, 0)
                total(0)
                if att:
                    dve.wait_ge(a_full, b * A_USES + A_QT + 1)
                    nc.vector.tensor_tensor(qt[:].rearrange("p (t i) -> p t i", t=NT),
                                            A(A_QT)[:, :].rearrange("p (t i) -> p t i", t=NT),
                                            rep(g_up, NT), ALU.mult).then_inc(dve_qt, 1)
                combine(1, 1)
                residual()
                combine(1, 2)
                ln2(0)
                combine(2, 0)
                total(1)
                ln2(1)
                k_decay(0)
                ln2(2)
                k_decay(1)
                combine(2, 1)
                k_decay(2)
                k_decay(3)
                ln2(3)
                combine(2, 2)
                combine(3, 0)
                total(2)
                combine(3, 1)
                combine(3, 2)
                if ffn:
                    dve.wait_ge(act_x2hi, f + 1)
                    low(x2T_lo[:], F(F_XT)[:, :], x2T_hi[:], dve_x2lo)
                total(3)
                scores(0, 0)
                scores(0, 1)
                route(0)
                scores(0, 2)
                route(1)
                route(2)
                state_add(0)
                route(3)
                state_mask(0)
                scores(1, 0)
                if ffn:
                    dve.wait_ge(f_full, f * F_USES + F_UP + 1)
                    dve.wait_ge(act_silu, f * SILU + 1)
                    nc.vector.tensor_tensor(hh[:, 8, :], F(F_UP)[:, :], gate[:], ALU.mult).then_inc(dve_up, 1)
                route(4)
                scores(1, 1)
                route(5)
                scores(1, 2)
                route(6)
                state_add(1)
                ln1(0)
                state_mask(1)
                scores(2, 0)
                ln1(1)
                scores(2, 1)
                ln1(2)
                scores(2, 2)
                route(7)
                state_add(2)
                route(8)
                state_mask(2)
                scores(3, 0)
                route(9)
                ln1(3)
                scores(3, 1)
                route(10)
                scores(3, 2)
                route(11)
                route(12)

            dve.wait_ge(x_loaded, 16)
            stats1(xin[:, 0], st1, ln1_step)
            stats2(0, st1, mv1, ln1_step)
            stats3(0, mv1, ve1, ln1_step, ln1_var)
            normalise(0, xn, xin[:, 0], mv1, rs1, ln1_rstd, xn_ready)
            wh = bass.AP(wqkv[:].tensor, 0, [list(wqkv[:].ap[0]), [HALF, 4], [0, 2], [1, HALF]])
            nc.vector.memset(rw_s[:].bitcast(f32), 0.0).then_inc(setup_hi, 1)
            dve.wait_ge(setup_hi, 1)
            dve.wait_ge(w_loaded, 16 * 8)
            nc.vector.tensor_copy(sel[:], mats[:, 5:9, :])
            nc.vector.tensor_copy(wh_hi[:], wh)
            nc.vector.tensor_copy(wqkv_hi[:], wqkv[:])
            nc.vector.tensor_copy(rw_s[:, 0:9], rw[:])
            nc.vector.tensor_copy(w1_hi[:], w1[:]).then_inc(setup_hi, 1)
            dve.wait_ge(setup_hi, 2)
            nc.vector.tensor_tensor(wh_lo[:], wh, wh_hi[:].bitcast(f32), ALU.subtract)
            nc.vector.tensor_tensor(wqkv_lo[:], wqkv[:], wqkv_hi[:].bitcast(f32), ALU.subtract)
            nc.vector.tensor_tensor(rw_s[:, 9:18], rw[:], rw_s[:, 0:9].bitcast(f32), ALU.subtract)
            nc.vector.tensor_tensor(w1_lo[:], w1[:], w1_hi[:].bitcast(f32), ALU.subtract).then_inc(setup_dve, 1)
            iterations(dve, steps)

        @block.tensor
        def _(pe):
            def tile(x, t):
                return x[:, t * P:t * P + P]

            def three(out, w_hi, w_lo, x_hi, x_lo):
                nc.tensor.matmul(out, w_hi, x_hi, start=True, stop=False)
                nc.tensor.matmul(out, w_hi, x_lo, start=False, stop=False)
                return nc.tensor.matmul(out, w_lo, x_hi, start=False, stop=True)

            def steps(b, p, att, ffn, moe, nxt):
                f, m = b - 1, b - 2

                def wait_a(u):
                    if u >= RA or later(b):
                        pe.wait_ge(*freed(A_FREED, RA, b, u))

                def wait_f(u):
                    if u >= RF or later(f):
                        pe.wait_ge(*freed(F_FREED, RF, f, u))

                def wait_m(u):
                    if u >= RM or later(m):
                        pe.wait_ge(*freed(M_FREED, RM, m, u))

                def half(n):
                    if att:
                        if n == 0:
                            pe.wait_ge(dve_xlo, b + 1)
                        wait_a(A_HALF + n)
                        three(A(A_HALF + n)[:, :], wh_hi[:, n].rearrange("p x c -> p (x c)"),
                              wh_lo[:, n].rearrange("p x c -> p (x c)"), xT_hi[:], xT_lo[:]).then_inc(a_full, 1)

                def q_terms(n):
                    if att:
                        wait_a(A_SELQ + n)
                        nc.tensor.matmul(A(A_SELQ + n)[:, :], sel[:, n % 2, :], halves[:, n // 2, :],
                                         start=True, stop=True).then_inc(a_full, 1)

                def k_terms(n):
                    if att:
                        pe.wait_ge(dve_half, b * 4 + 2 + n // 2 + 1)
                        wait_a(A_SELK + n)
                        nc.tensor.matmul(A(A_SELK + n)[:, :], sel[:, 2 + n % 2, :], halves[:, 2 + n // 2, :],
                                         start=True, stop=True).then_inc(a_full, 1)

                def kv(t):
                    if att:
                        wait_a(A_KV + t)
                        three(A(A_KV + t)[:, 0:2 * C], tile(xT_hi, t), tile(xT_lo, t), wqkv_hi[:, C:3 * C],
                              wqkv_lo[:, C:3 * C]).then_inc(a_full, 1)

                def scores(t, q):
                    if att:
                        if t == 0 and q == 0:
                            pe.wait_ge(q_spread, b * 16 * HQ + 16 * HQ)
                        wait_a(a_s(t, q))
                        nc.tensor.matmul(A(a_s(t, q))[:, :], tile(k4[:, q, :], t),
                                         qbd[:, q, t].rearrange("p h i -> p (h i)"),
                                         start=True, stop=True).then_inc(a_full, 1)

                def update(t):
                    if att:
                        pe.wait_ge(dve_kt, b * NT + t + 1)
                        wait_a(a_u(t))
                        nc.tensor.matmul(A(a_u(t))[:, 0:C], kt[:, t, :], diag(t), start=True,
                                         stop=True).then_inc(a_full, 1)

                def values(t):
                    if not att:
                        return
                    if t == 0:
                        pe.wait_ge(act_v, b * NT + NT)
                        if later(b):
                            pe.wait_ge(act_yn, b)
                    else:
                        pe.wait_ge(dve_statem, b * (NT - 1) + t)
                        nc.tensor.matmul(tile(bankY, t), state_m[:, t - 1, :], tile(qt, t), start=True, stop=False,
                                         skip_group_check=True)
                    pe.wait_ge(dve_s, b * DQ * NT + DQ * t + DQ)
                    pe.wait_ge(pool_s, b * NT + t + 1)
                    for h in range(HQ):
                        for q in range(NQ):
                            rows = slice(32 * q, 32 * q + 32)
                            last = nc.tensor.matmul(bankY[rows, t * P:t * P + P], vbd[:, t, h, rows],
                                                    sm[:, t % 2, q, h * P:h * P + P],
                                                    start=(t == 0 and h == 0), stop=(h == HQ - 1),
                                                    skip_group_check=True)
                    last.then_inc(y_full, 1)

                def up(u):
                    if ffn:
                        n = {F_GATE: 8, F_UP: 9}.get(u, u - F_EXP)
                        wait_f(u)
                        three(F(u)[:, :], w1_hi[:, n * C:n * C + C], w1_lo[:, n * C:n * C + C], x2T_hi[:],
                              x2T_lo[:]).then_inc(f_full, 1)

                def down(t, g):
                    if moe:
                        if t == 0 and g == 0:
                            pe.wait_ge(act_silu, m * SILU + SILU)
                            pe.wait_ge(dve_up, m + 1)
                        wait_m(3 * t + g)
                        for e in GROUPS[g]:
                            last = nc.tensor.matmul(M(3 * t + g)[:, (e % 4) * C:(e % 4) * C + C],
                                                    tile(hh[:, e, :], t), w2[:, e * C:e * C + C],
                                                    start=True, stop=True)
                        last.then_inc(m_full, 1)

                if att:
                    pe.wait_ge(xn_ready, b + 1)
                    wait_a(A_XT)
                    for t in range(NT):
                        last = nc.tensor.transpose(tile(A(A_XT), t), xn[:, t, :], ident)
                    last.then_inc(a_full, 1)
                down(0, 0)
                half(0)
                half(1)
                if ffn:
                    pe.wait_ge(gn_stats, f + 1)
                    wait_f(F_GN)
                    nc.tensor.matmul(F(F_GN)[:, 0:2], avg8, gmv[:], start=True, stop=True).then_inc(f_full, 1)
                down(0, 1)
                half(2)
                down(0, 2)
                half(3)
                down(1, 0)
                if att:
                    wait_a(A_QT)
                    three(A(A_QT)[:, :], wqkv_hi[:, 0:C], wqkv_lo[:, 0:C], xT_hi[:], xT_lo[:]).then_inc(a_full, 1)
                down(1, 1)
                if ffn:
                    pe.wait_ge(act_yn, f + 1)
                    wait_f(F_OUT)
                    for t in range(NT):
                        last = nc.tensor.matmul(tile(F(F_OUT), t), tile(yn, t), wo[:], start=True, stop=True)
                    last.then_inc(f_full, 1)
                q_terms(0)
                q_terms(1)
                down(1, 2)
                q_terms(2)
                q_terms(3)
                down(2, 0)
                kv(0)
                kv(1)
                down(2, 1)
                kv(2)
                kv(3)
                down(2, 2)
                k_terms(0)
                down(3, 0)
                k_terms(1)
                down(3, 1)
                k_terms(2)
                down(3, 2)
                k_terms(3)
                if ffn:
                    pe.wait_ge(x2n_ready, f + 1)
                    wait_f(F_XT)
                    for t in range(NT):
                        last = nc.tensor.transpose(tile(F(F_XT), t), x2n[:, t, :], ident)
                    last.then_inc(f_full, 1)
                scores(0, 0)
                scores(0, 1)
                if ffn:
                    pe.wait_ge(dve_x2lo, f + 1)
                    wait_f(F_LG)
                    for t in range(NT):
                        lgs = F(F_LG)[:, 32 * t:32 * t + 2 * C]
                        nc.tensor.matmul(lgs, tile(x2T_hi, t), rw_s[:], start=True, stop=False,
                                         skip_group_check=True)
                        last = nc.tensor.matmul(lgs, tile(x2T_lo, t), rw_s[:], start=False, stop=True,
                                                skip_group_check=True)
                    last.then_inc(f_full, 1)
                scores(0, 2)
                scores(0, 3)
                up(F_GATE)
                update(0)
                up(F_UP)
                scores(1, 0)
                up(F_EXP + 0)
                scores(1, 1)
                values(0)
                scores(1, 2)
                up(F_EXP + 1)
                scores(1, 3)
                update(1)
                up(F_EXP + 2)
                scores(2, 0)
                values(1)
                scores(2, 1)
                up(F_EXP + 3)
                scores(2, 2)
                up(F_EXP + 4)
                scores(2, 3)
                update(2)
                scores(3, 0)
                values(2)
                scores(3, 1)
                up(F_EXP + 5)
                scores(3, 2)
                up(F_EXP + 6)
                scores(3, 3)
                up(F_EXP + 7)
                values(3)

            pe.wait_ge(w_loaded, 16 * 8)
            pe.wait_ge(setup_dve, 1)
            pe.wait_ge(setup_pool, 3)
            iterations(pe, steps)


def constants():
    import numpy as np
    lo, hi = np.float32(np.log(1.0 - 0.999)), np.float32(np.log(1.0 - 0.9))
    gamma = (np.float32(1) - np.exp(np.linspace(lo, hi, H, dtype=np.float32))).astype(np.float64)
    i = np.arange(P)
    dist = i[None, :] - i[:, None]
    decay = np.where(dist[:, None, :] >= 0, gamma[None, :, None] ** np.maximum(dist, 0)[:, None, :], 0.0)
    gp = np.repeat(gamma, HD)
    head = np.arange(C) // HD
    mats = np.zeros((P, 10, P))
    mats[:, 0] = np.eye(P)
    mats[:, 1] = gp[:, None] ** (i[None, :] + 1)
    mats[:, 2] = gp[None, :] ** (P - 1 - i[:, None])
    mats[:, 3] = head[:, None] == head[None, :]
    mats[:, 4] = (head[:, None] == head[None, :]) / HD
    for which, parts in enumerate(((0, 1, 0, 1), (0, 0, 1, 1))):
        for n in range(2):
            for h in range(HQ):
                for term, part in enumerate(parts):
                    for a in range(HD):
                        mats[part * HALF + (HQ * n + h) * HD + a, 5 + 2 * which + n, h * 32 + term * HD + a] = 1
    mats[:, 9, 0] = gp ** P
    mats[:, 9, 8:8 + E] = np.arange(E)
    return decay.astype(np.float32), mats.astype(np.float32)


def kernel(**inputs):
    import numpy as np
    import concourse.bacc as bacc
    from concourse import mybir as mb
    from concourse.bass_utils import run_bass_kernel_spmd

    g = {k.split("_", 1)[1]: np.asarray(v) for k, v in inputs.items()}
    decay, mats = constants()

    def columns(w):
        return np.transpose(w, (1, 0, 2)).reshape(w.shape[1], -1)

    arrays = {
        "x": g["attn_x"],
        "wqkv": np.concatenate([g["attn_wq"].T, g["attn_wk"].T, g["attn_wv"].T], axis=1),
        "wo": g["attn_wo"].T,
        "w1": np.concatenate([columns(g["ffn_w1"]), g["ffn_shared_gate_up"]], axis=1),
        "w2": np.concatenate([columns(g["ffn_w2"]), g["ffn_shared_down"]], axis=1),
        "rw": np.concatenate([g["ffn_router_w"], g["ffn_shared_gate_w"]], axis=1),
        "gn": np.stack([g["attn_gn_w"], g["attn_gn_b"]], axis=1),
        "decay": decay,
        "mats": mats,
    }
    arrays = {f"in_{k}": np.ascontiguousarray(v) for k, v in arrays.items()}
    nc = bacc.Bacc("TRN2", target_bir_lowering=False, num_devices=1)
    args = [nc.dram_tensor(k, v.shape, mb.dt.from_np(v.dtype), kind="ExternalInput").ap() for k, v in arrays.items()]
    out = nc.dram_tensor("out", (B, T, C), mb.dt.float32, kind="ExternalOutput").ap()
    preln_layer_kernel(nc, *args, out)
    r = run_bass_kernel_spmd(nc, [arrays], core_ids=[0])
    return r.results[0]["out"]
```

```python
import concourse.bass as bass
from concourse import mybir
from contextlib import ExitStack

B, T, C = 16, 512, 128
H, HD = 16, 8
E = 8
P = 128
NT = T // P
HQ = 4
NQ = H // HQ
HALF = C // 2
EPS = 1e-5

RA = 3
A_XT, A_HALF, A_SELQ, A_QT, A_KV, A_SELK, A_TILE = 0, 1, (5, 6, 8, 9), 7, 10, 12, 16
A_USES = A_TILE + 5 * NT - 1
F_GN, F_OUT, F_XT, F_LG, F_GATE, F_UP, F_EXP, F_USES = 0, 1, 2, 3, 4, 5, 6, 14
M_USES = 3 * NT
GROUPS = [(0, 1, 2, 3), (4, 5), (6, 7, 8)]
RG = 4
G_ORDER = ([("m", 0), ("m", 1), ("m", 2), ("f", F_GN), ("m", 3), ("m", 4), ("f", F_OUT)]
           + [("m", u) for u in range(5, 10)] + [("f", F_XT), ("m", 10), ("m", 11)]
           + [("f", u) for u in range(F_LG, F_USES)])
G_USES = len(G_ORDER)
LAG = {"f": 1, "m": 2}
DQ = 3
QUADS = [3, 0, 1, 2]
SILU = 9
MOE = 6
ROUTE = 13


def a_s(t, q):
    return A_TILE + 5 * t + QUADS.index(q)


def a_u(t):
    return A_TILE + 5 * t + 4


def later(b):
    return not isinstance(b, int) or b > 0


def preln_layer_kernel(nc, x_d, wqkv_d, wo_d, w1_d, w2_d, rw_d, gn_d, decay_d, mats_d, out_d):
    f32 = mybir.dt.float32
    f32r = mybir.dt.float32r
    ALU = mybir.AluOpType
    ACT = mybir.ActivationFunctionType
    AX = mybir.AxisListType

    x_v = x_d.rearrange("b (t p) c -> b p t c", p=P)
    out_v = out_d.rearrange("b (t p) c -> b p t c", p=P)

    ctx = ExitStack()
    with ctx:
        def sb(name, shape, dt=f32):
            return ctx.enter_context(nc.sbuf_tensor(name, shape, dt))

        def sem(name):
            return ctx.enter_context(nc.semaphore(name))

        decay = sb("decay", [P, H, P])
        mats = sb("mats", [P, 10, P])
        ident, g_up, g_down, bdmask, avg8 = (mats[:, n, :] for n in range(5))
        gC, iota = mats[:, 9, 0:1], mats[:, 9, 8:8 + E]
        sel = sb("sel", [P, 4, P], f32r)
        gnp = sb("gnp", [P, 2])
        wqkv = sb("wqkv", [P, 3 * C])
        wo = sb("wo", [P, C])
        w1 = sb("w1", [P, 10 * C])
        w2 = sb("w2", [P, 9 * C])
        rw = sb("rw", [P, 9])
        wh_hi = sb("wh_hi", [P, 4, 2, HALF], f32r)
        wh_lo = sb("wh_lo", [P, 4, 2, HALF], f32r)
        wqkv_hi = sb("wqkv_hi", [P, 3 * C], f32r)
        wqkv_lo = sb("wqkv_lo", [P, 3 * C], f32r)
        w1_hi = sb("w1_hi", [P, 10 * C], f32r)
        w1_lo = sb("w1_lo", [P, 10 * C], f32r)
        rw_s = sb("rw_s", [P, 2 * C], f32r)
        xin = sb("xin", [P, 2, NT, C])
        xn = sb("xn", [P, NT, C])
        xT_hi = sb("xT_hi", [P, T], f32r)
        xT_lo = sb("xT_lo", [P, T], f32r)
        halves = sb("halves", [P, 4, T], f32r)
        qt = sb("qt", [P, T])
        q4 = sb("q4", [P, NQ, T], f32r)
        k4 = sb("k4", [P, NQ, T], f32r)
        qbd = sb("qbd", [P, NQ, NT, HQ, P], f32r)
        kt = sb("kt", [P, NT, C])
        vbd = sb("vbd", [P, NT, HQ, C])
        sm = sb("sm", [P, 2, NQ, HQ * P])
        s_raw = sb("s_raw", [P, 2, HQ * P])
        state = sb("state", [P, C])
        state_m = sb("state_m", [P, NT - 1, C])
        yn = sb("yn", [P, T])
        st1 = sb("st1", [P, NT, 6])
        mv1 = sb("mv1", [P, NT, 2])
        ve1 = sb("ve1", [P, NT])
        rs1 = sb("rs1", [P, NT])
        gst = sb("gst", [P, 6])
        gmv = sb("gmv", [P, 2])
        gm = sb("gm", [P, 2])
        gvar = sb("gvar", [P, 1])
        gve = sb("gve", [P, 1])
        grs = sb("grs", [P, 1])
        gab = sb("gab", [P, 2])
        mhalf = sb("mhalf", [P, NT])
        res = sb("res", [P, 2, NT, C])
        st2 = sb("st2", [P, NT, 6])
        mv2 = sb("mv2", [P, NT, 2])
        ve2 = sb("ve2", [P, NT])
        rs2 = sb("rs2", [P, NT])
        x2n = sb("x2n", [P, NT, C])
        x2T_hi = sb("x2T_hi", [P, T], f32r)
        x2T_lo = sb("x2T_lo", [P, T], f32r)
        lgc = sb("lgc", [P, NT, 18])
        lg = sb("lg", [P, NT, 9])
        mx = sb("mx", [P, NT, 8])
        ix = sb("ix", [P, NT, 8], mybir.dt.uint32)
        dd = sb("dd", [P, NT, 9])
        ee = sb("ee", [P, NT, 9])
        m0 = sb("m0", [P, NT, 8])
        m1 = sb("m1", [P, NT, 8])
        den = sb("den", [P, NT, 2])
        rden = sb("rden", [P, NT, 2])
        em = sb("em", [P, NT, 8])
        cw = sb("cw", [P, NT, 9])
        gate = sb("gate", [P, T])
        hh = sb("hh", [P, 9, T])
        carrier = sb("carrier", [P, 1])
        nb2 = sb("nb2", [P, NT])
        accs = sb("accs", [P, 2, 4, C])
        warm = sb("warm", [P, 1])

        bankA = [ctx.enter_context(nc.psum_tensor(f"bankA{i}", [P, 512], f32)) for i in range(RA)]
        bankY = ctx.enter_context(nc.psum_tensor("bankY", [P, T], f32))
        bankG = [ctx.enter_context(nc.psum_tensor(f"bankG{i}", [P, 512], f32)) for i in range(RG)]

        def A(u):
            return bankA[u % RA]

        def G(what, p, u):
            return bankG[(p * G_USES + G_ORDER.index((what, u))) % RG]

        def diag(t):
            v = vbd[:, t, 0, :]
            return bass.AP(v.tensor, v.offset, [list(v.ap[0]), [HQ * HD, NQ], [C + HD, HQ], [1, HD]])

        def per(v, n):
            return bass.AP(v.tensor, v.offset, [list(p) for p in v.ap] + [[0, n]])

        def rep(v, n):
            return bass.AP(v.tensor, v.offset, [list(v.ap[0]), [0, n]] + [list(p) for p in v.ap[1:]])

        w_loaded = sem("w_loaded")
        x_loaded = sem("x_loaded")
        q_spread = sem("q_spread")
        out_stored = sem("out_stored")
        setup_pool = sem("setup_pool")
        setup_hi = sem("setup_hi")
        setup_dve = sem("setup_dve")
        ln1_rstd = sem("ln1_rstd")
        ln2_rstd = sem("ln2_rstd")
        gn_rstd = sem("gn_rstd")
        pool_s = sem("pool_s")
        a_full = sem("a_full")
        f_full = sem("f_full")
        m_full = sem("m_full")
        y_full = sem("y_full")
        act_xhi = sem("act_xhi")
        act_half = sem("act_half")
        act_q4 = sem("act_q4")
        act_k4 = sem("act_k4")
        act_v = sem("act_v")
        act_s = sem("act_s")
        act_yn = sem("act_yn")
        act_x2n = sem("act_x2n")
        act_x2hi = sem("act_x2hi")
        act_lg = sem("act_lg")
        act_exp = sem("act_exp")
        act_silu = sem("act_silu")
        ln1_step = sem("ln1_step")
        ln1_var = sem("ln1_var")
        xn_ready = sem("xn_ready")
        dve_xlo = sem("dve_xlo")
        dve_half = sem("dve_half")
        dve_qt = sem("dve_qt")
        dve_kt = sem("dve_kt")
        dve_s = sem("dve_s")
        dve_state = sem("dve_state")
        dve_statem = sem("dve_statem")
        gn_step = sem("gn_step")
        gn_stats = sem("gn_stats")
        gn_mean = sem("gn_mean")
        gn_diff = sem("gn_diff")
        gn_var = sem("gn_var")
        gn_scale = sem("gn_scale")
        gn_ab = sem("gn_ab")
        dve_x1 = sem("dve_x1")
        ln2_step = sem("ln2_step")
        ln2_var = sem("ln2_var")
        dve_x2n = sem("dve_x2n")
        dve_x2lo = sem("dve_x2lo")
        dve_route = sem("dve_route")
        dve_up = sem("dve_up")
        dve_moe = sem("dve_moe")
        pool_moe = sem("pool_moe")
        pool_out = sem("pool_out")
        act_moe = sem("act_moe")
        act_warm = sem("act_warm")
        ln2_bias = sem("ln2_bias")
        decay_loaded = sem("decay_loaded")
        wf_loaded = sem("wf_loaded")
        setup_ffn_hi = sem("setup_ffn_hi")
        setup_ffn = sem("setup_ffn")

        A_FREED = [(dve_xlo, 1, 1)] + [(dve_half, 4, n + 1) for n in range(4)]
        A_FREED += [(act_q4, NQ, 1), (act_q4, NQ, 2), (dve_qt, 1, 1), (act_q4, NQ, 3), (act_q4, NQ, 4)]
        A_FREED += [(dve_kt, NT // 2, n + 1) for n in range(NT // 2)]
        A_FREED += [(act_k4, NQ, n + 1) for n in range(NQ)]
        for t in range(NT):
            A_FREED += [(act_s, NT, t + 1)] + [(dve_s, DQ * NT, DQ * t + q + 1) for q in range(DQ)]
            A_FREED += [(dve_state, NT - 1, t + 1)] if t < NT - 1 else []
        F_FREED = [(gn_mean, 1, 1), (dve_x1, 1, 1), (dve_x2lo, 1, 1), (act_lg, 1, 1), (act_silu, SILU, 1),
                   (dve_up, 1, 1)] + [(act_silu, SILU, 2 + e) for e in range(E)]
        M_FREED = [(dve_moe, MOE * NT, MOE * t + g) for t in range(NT) for g in (4, 6, 0)]
        M_FREED[2::3] = [(act_moe, 3 * NT, 3 * t + 3) for t in range(NT)]
        assert len(A_FREED) == A_USES and len(F_FREED) == F_USES and len(M_FREED) == M_USES

        def freed_a(b, u):
            s, per_seq, k = A_FREED[u - RA]
            return s, (b if u >= RA else b - 1) * per_seq + k

        def freed_g(b, what, u):
            at = G_ORDER.index((what, u)) - RG
            while True:
                if at < 0:
                    at, b = at + G_USES, b - 1
                was, v = G_ORDER[at]
                if not isinstance(b, int) or 0 <= b - LAG[was] < B:
                    s, per_seq, k = (F_FREED if was == "f" else M_FREED)[v]
                    return s, (b - LAG[was]) * per_seq + k
                if b < 0:
                    return None
                at -= RG

        def sequence(dram, b):
            return dram[b] if isinstance(b, int) else dram[bass.ds(b, 1)].rearrange("o p t c -> (o p) t c")

        block = ctx.enter_context(nc.Block())

        def iterations(eng, steps):
            steps(0, 0, True, False, False, True)
            steps(1, 1, True, True, False, True)
            steps(2, 0, True, True, True, True)
            with eng.Fori(0, (B - 4) // 2) as k:
                steps(2 * k + 3, 1, True, True, True, True)
                steps(2 * k + 4, 0, True, True, True, True)
            steps(B - 1, 1, True, True, True, False)
            steps(B, 0, False, True, True, False)
            steps(B + 1, 1, False, False, True, False)

        @block.sync
        def _(sp):
            sp.dma_start(xin[:, 0], x_v[0]).then_inc(x_loaded, 16)
            sp.dma_start(wqkv[:], wqkv_d).then_inc(w_loaded, 16)
            sp.dma_start(mats[:], mats_d).then_inc(w_loaded, 16)
            sp.dma_start(decay[:], decay_d).then_inc(decay_loaded, 16)
            for dst, src in ((gnp[:], gn_d), (wo[:], wo_d), (rw[:], rw_d), (w1[:], w1_d), (w2[:], w2_d)):
                sp.dma_start(dst, src).then_inc(wf_loaded, 16)
            sp.wait_ge(setup_pool, 2)

            def steps(b, p, att, ffn, moe, nxt):
                if nxt:
                    if later(b):
                        sp.wait_ge(dve_x1, b)
                    else:
                        sp.wait_ge(ln1_step, 1)
                    sp.dma_start(xin[:, 1 - p], sequence(x_v, b + 1)).then_inc(x_loaded, 16)
                if att:
                    sp.wait_ge(act_q4, b * NQ + NQ)
                    if later(b):
                        sp.wait_ge(a_full, (b - 1) * A_USES + A_USES)
                    for h in range(HQ):
                        rows = slice(32 * h, 32 * h + 32)
                        sp.dma_start(qbd[rows, :, :, h, :].bitcast(f32),
                                     q4[rows, :, :].rearrange("p q (t i) -> p q t i", t=NT).bitcast(f32)
                                     ).then_inc(q_spread, 16)
                if moe:
                    sp.wait_ge(pool_out, (b - 2) * NT + NT)
                    sp.dma_start(sequence(out_v, b - 2), res[:, p]).then_inc(out_stored, 16)

            iterations(sp, steps)
            sp.wait_ge(out_stored, 16 * B)

        @block.gpsimd
        def _(pool):
            nc.gpsimd.memset(mhalf[:], -0.5).then_inc(setup_pool, 1)
            nc.gpsimd.memset(qbd[:].bitcast(f32), 0.0).then_inc(setup_pool, 1)
            nc.gpsimd.memset(vbd[:], 0.0).then_inc(setup_pool, 1)
            pool.wait_ge(setup_pool, 1)
            pool.wait_ge(ln1_var, 1)
            nc.gpsimd.tensor_tensor(rs1[:], ve1[:], mhalf[:], ALU.pow).then_inc(ln1_rstd, 1)
            pool.wait_ge(decay_loaded, 16)

            def steps(b, p, att, ffn, moe, nxt):
                f, m = b - 1, b - 2

                def total(t):
                    if moe:
                        acc = accs[:, t % 2]
                        pool.wait_ge(act_moe, m * 3 * NT + 3 * t + 3)
                        pool.wait_ge(dve_moe, m * MOE * NT + MOE * t + MOE)
                        nc.gpsimd.tensor_tensor(acc[:, 0:2, :], acc[:, 0:2, :], acc[:, 2:4, :],
                                                ALU.add).then_inc(pool_moe, 1)
                        pool.wait_ge(pool_moe, m * 2 * NT + 2 * t + 1)
                        nc.gpsimd.tensor_tensor(acc[:, 0, :], acc[:, 0, :], acc[:, 1, :],
                                                ALU.add).then_inc(pool_moe, 1)
                        pool.wait_ge(pool_moe, m * 2 * NT + 2 * t + 2)
                        nc.gpsimd.tensor_tensor(res[:, p, t, :], res[:, p, t, :], acc[:, 0, :],
                                                ALU.add).then_inc(pool_out, 1)

                def scores(t):
                    if att:
                        pool.wait_ge(act_s, b * NT + t + 1)
                        nc.gpsimd.tensor_tensor(sm[:, t % 2, DQ, :], s_raw[:, t % 2, :],
                                                decay[:, HQ * DQ:, :].rearrange("p h i -> p (h i)"),
                                                ALU.mult).then_inc(pool_s, 1)

                if ffn:
                    pool.wait_ge(gn_var, f + 1)
                    nc.gpsimd.tensor_tensor(grs[:], gve[:], mhalf[:, 0:1], ALU.pow).then_inc(gn_rstd, 1)
                total(0)
                if ffn:
                    pool.wait_ge(ln2_var, f + 1)
                    nc.gpsimd.tensor_tensor(rs2[:], ve2[:], mhalf[:], ALU.pow).then_inc(ln2_rstd, 1)
                total(1)
                total(2)
                total(3)
                scores(0)
                scores(1)
                scores(2)
                if nxt:
                    pool.wait_ge(ln1_var, b + 2)
                    nc.gpsimd.tensor_tensor(rs1[:], ve1[:], mhalf[:], ALU.pow).then_inc(ln1_rstd, 1)
                scores(3)

            iterations(pool, steps)

        @block.scalar
        def _(act):
            def copy(out, in_):
                return nc.scalar.activation(out, in_, ACT.Copy)

            def steps(b, p, att, ffn, moe, nxt):
                f, m = b - 1, b - 2

                def half(n):
                    if att:
                        act.wait_ge(a_full, b * A_USES + A_HALF + n + 1)
                        copy(halves[:, n, :], A(A_HALF + n)[:, :]).then_inc(act_half, 1)

                def q_terms(n):
                    if att:
                        act.wait_ge(a_full, b * A_USES + A_SELQ[n] + 1)
                        if n == 0 and later(b):
                            act.wait_ge(q_spread, (b - 1) * 16 * HQ + 16 * HQ)
                        copy(q4[:, n, :], A(A_SELQ[n])[:, :]).then_inc(act_q4, 1)

                def k_terms(n):
                    if att:
                        act.wait_ge(a_full, b * A_USES + A_SELK + n + 1)
                        copy(k4[:, QUADS[n], :], A(A_SELK + n)[:, :]).then_inc(act_k4, 1)

                def values(n):
                    if att:
                        act.wait_ge(a_full, b * A_USES + A_KV + n + 1)
                        for t in (0, 1):
                            v = A(A_KV + n)[:, t * 2 * C + C:t * 2 * C + 2 * C]
                            copy(diag(2 * n + t), v.rearrange("p (q h c) -> p q h c", q=NQ, h=HQ)).then_inc(act_v, 1)

                def weigh(t):
                    if moe:
                        act.wait_ge(m_full, m * M_USES + 3 * t + 3)
                        if t == 0:
                            act.wait_ge(dve_route, m * ROUTE + ROUTE)
                        if t >= 2 or later(m):
                            act.wait_ge(pool_out, m * NT + t - 1)
                        for n, e in enumerate(GROUPS[2]):
                            nc.scalar.activation(accs[:, t % 2, n, :], G("m", p, 3 * t + 2)[:, n * C:n * C + C], ACT.Copy,
                                                 scale=cw[:, t, e:e + 1]).then_inc(act_moe, 1)

                def scores(t):
                    if att:
                        act.wait_ge(a_full, b * A_USES + a_s(t, DQ) + 1)
                        if t >= 2 or later(b):
                            act.wait_ge(pool_s, b * NT + t - 1)
                        copy(s_raw[:, t % 2, :], A(a_s(t, DQ))[:, :]).then_inc(act_s, 1)

                def silu(e):
                    if ffn:
                        act.wait_ge(f_full, f * F_USES + F_EXP + e + 1)
                        nc.scalar.activation(hh[:, e, :], G("f", p, F_EXP + e)[:, :], ACT.Silu).then_inc(act_silu, 1)

                if att:
                    act.wait_ge(a_full, b * A_USES + A_XT + 1)
                    copy(xT_hi[:], A(A_XT)[:, :]).then_inc(act_xhi, 1)
                half(0)
                half(1)
                weigh(0)
                half(2)
                if ffn:
                    act.wait_ge(gn_ab, f + 1)
                    nc.scalar.activation(yn[:], bankY[:, :], ACT.Identity, scale=gab[:, 0:1],
                                         bias=gab[:, 1:2]).then_inc(act_yn, 1)
                half(3)
                q_terms(0)
                q_terms(1)
                q_terms(2)
                q_terms(3)
                weigh(1)
                values(0)
                values(1)
                if ffn:
                    act.wait_ge(ln2_bias, f + 1)
                    for t in (0, 1):
                        last = nc.scalar.activation(x2n[:, t, :], res[:, 1 - p, t, :], ACT.Identity,
                                                    scale=rs2[:, t:t + 1], bias=nb2[:, t:t + 1])
                    last.then_inc(act_x2n, 1)
                k_terms(0)
                weigh(2)
                k_terms(1)
                if ffn:
                    act.wait_ge(f_full, f * F_USES + F_XT + 1)
                    copy(x2T_hi[:], G("f", p, F_XT)[:, :]).then_inc(act_x2hi, 1)
                k_terms(2)
                k_terms(3)
                scores(0)
                weigh(3)
                if ffn:
                    nc.scalar.activation(warm[:], gnp[:, 0:1], ACT.Exp).then_inc(act_warm, 1)
                    act.wait_ge(f_full, f * F_USES + F_LG + 1)
                    if later(f):
                        act.wait_ge(dve_route, (f - 1) * ROUTE + 1)
                    copy(lgc[:], G("f", p, F_LG)[:, 0:32 * NT].rearrange("p (t c) -> p t c", t=NT)[:, :, 0:18]
                         ).then_inc(act_lg, 1)
                scores(1)
                if ffn:
                    act.wait_ge(dve_route, f * ROUTE + 3)
                    nc.scalar.activation(ee[:], dd[:], ACT.Exp).then_inc(act_exp, 1)
                    act.wait_ge(f_full, f * F_USES + F_GATE + 1)
                    if later(f):
                        act.wait_ge(dve_up, f)
                    nc.scalar.activation(gate[:], G("f", p, F_GATE)[:, :], ACT.Silu).then_inc(act_silu, 1)
                silu(0)
                silu(1)
                scores(2)
                silu(2)
                silu(3)
                scores(3)
                silu(4)
                silu(5)
                silu(6)
                silu(7)

            act.wait_ge(setup_pool, 3)
            iterations(act, steps)

        @block.vector
        def _(dve):
            def low(dst, full, hi, ready):
                nc.vector.tensor_tensor(dst, full, hi.bitcast(f32), ALU.subtract).then_inc(ready, 1)

            def stats1(src, st, step):
                for t in range(NT):
                    last = nc.vector.bn_stats(st[:, t, :], src[:, t, :])
                last.then_inc(step, 1)

            def stats2(b, st, mv, step):
                dve.wait_ge(step, 2 * b + 1)
                nc.vector.memset(carrier[:], 0.0)
                for t in range(NT):
                    last = nc.vector.bn_aggr(mv[:, t, :], st[:, t, :])
                last.then_inc(step, 1)

            def stats3(b, mv, ve, step, var):
                dve.wait_ge(step, 2 * b + 2)
                nc.vector.tensor_scalar(ve[:], mv[:, :, 1], EPS, None, ALU.add).then_inc(var, 1)

            def normalise(b, dst, src, mv, rs, rstd, ready):
                dve.wait_ge(rstd, b + 1)
                for t in range(NT):
                    last = nc.vector.tensor_scalar(dst[:, t, :], src[:, t, :], mv[:, t, 0:1], rs[:, t:t + 1],
                                                   ALU.subtract, ALU.mult)
                last.then_inc(ready, 1)

            def steps(b, p, att, ffn, moe, nxt):
                f, m, pf = b - 1, b - 2, 1 - p

                def half(n):
                    if att:
                        dve.wait_ge(act_half, b * 4 + n + 1)
                        low(halves[HALF:, n, :], A(A_HALF + n)[HALF:, :], halves[HALF:, n, :], dve_half)

                def k_decay(n):
                    if att:
                        dve.wait_ge(act_v, b * NT + 2 * n + 2)
                        nc.vector.tensor_tensor(kt[:, 2 * n:2 * n + 2, :],
                                                A(A_KV + n)[:, :].rearrange("p (t c) -> p t c", t=2)[:, :, 0:C],
                                                rep(g_down, 2), ALU.mult).then_inc(dve_kt, 1)

                def scores(t, q):
                    if att:
                        if not later(b) and t == 0 and q == 0:
                            dve.wait_ge(decay_loaded, 16)
                        dve.wait_ge(a_full, b * A_USES + a_s(t, q) + 1)
                        nc.vector.tensor_tensor(sm[:, t % 2, q, :].rearrange("p (h i) -> p h i", h=HQ),
                                                A(a_s(t, q))[:, :].rearrange("p (h i) -> p h i", h=HQ),
                                                decay[:, HQ * q:HQ * q + HQ, :], ALU.mult).then_inc(dve_s, 1)

                def state_add(t):
                    if att:
                        dve.wait_ge(a_full, b * A_USES + a_u(t) + 1)
                        if t == 0:
                            nc.vector.tensor_copy(state[:], A(a_u(t))[:, 0:C]).then_inc(dve_state, 1)
                        else:
                            nc.vector.scalar_tensor_tensor(state[:], state[:], gC, A(a_u(t))[:, 0:C],
                                                           ALU.mult, ALU.add).then_inc(dve_state, 1)

                def state_mask(t):
                    if att:
                        dve.wait_ge(dve_state, b * (NT - 1) + t + 1)
                        nc.vector.tensor_tensor(state_m[:, t, :], state[:], bdmask, ALU.mult).then_inc(dve_statem, 1)

                def combine(t, g):
                    if not moe:
                        return
                    dve.wait_ge(m_full, m * M_USES + 3 * t + g + 1)
                    for n, e in enumerate(GROUPS[g]):
                        y, w = G("m", p, 3 * t + g)[:, n * C:n * C + C], cw[:, t, e:e + 1]
                        acc = accs[:, t % 2, 3, :] if e % 2 else res[:, p, t, :]
                        if e >= 2:
                            dve.wait_ge(dve_moe, m * MOE * NT + MOE * t + e - 1)
                        if e == 1:
                            if t >= 2 or later(m):
                                dve.wait_ge(pool_out, m * NT + t - 1)
                            nc.vector.tensor_scalar(acc, y, w, None, ALU.mult).then_inc(dve_moe, 1)
                        else:
                            nc.vector.scalar_tensor_tensor(acc, y, w, acc, ALU.mult, ALU.add).then_inc(dve_moe, 1)

                def gn_sums():
                    if ffn:
                        dve.wait_ge(y_full, f * NT + NT)
                        nc.vector.bn_stats(gst[:], bankY[:, :]).then_inc(gn_step, 1)
                        dve.wait_ge(gn_step, 2 * f + 1)
                        nc.vector.memset(carrier[:], 0.0)
                        nc.vector.bn_aggr(gmv[:], gst[:]).then_inc(gn_step, 1)

                def gn_square():
                    if ffn:
                        dve.wait_ge(gn_step, 2 * f + 2)
                        nc.vector.scalar_tensor_tensor(gmv[:, 1:2], gmv[:, 0:1], gmv[:, 0:1], gmv[:, 1:2],
                                                       ALU.mult, ALU.add).then_inc(gn_stats, 1)

                def gn_variance():
                    if ffn:
                        dve.wait_ge(f_full, f * F_USES + F_GN + 1)
                        nc.vector.tensor_copy(gm[:], G("f", p, F_GN)[:, 0:2]).then_inc(gn_mean, 1)
                        dve.wait_ge(gn_mean, f + 1)
                        nc.vector.scalar_tensor_tensor(gvar[:], gm[:, 0:1], gm[:, 0:1], gm[:, 1:2], ALU.mult,
                                                       ALU.subtract, reverse1=True).then_inc(gn_diff, 1)
                        dve.wait_ge(gn_diff, f + 1)
                        nc.vector.tensor_scalar(gve[:], gvar[:], 0.0, EPS, ALU.max, ALU.add).then_inc(gn_var, 1)

                def gn_affine():
                    if ffn:
                        dve.wait_ge(gn_rstd, f + 1)
                        nc.vector.tensor_tensor(gab[:, 0:1], grs[:], gnp[:, 0:1], ALU.mult).then_inc(gn_scale, 1)
                        dve.wait_ge(gn_scale, f + 1)
                        nc.vector.scalar_tensor_tensor(gab[:, 1:2], gm[:, 0:1], gab[:, 0:1], gnp[:, 1:2], ALU.mult,
                                                       ALU.subtract, reverse1=True).then_inc(gn_ab, 1)

                def residual():
                    if ffn:
                        dve.wait_ge(f_full, f * F_USES + F_OUT + 1)
                        if not isinstance(b, int) or f >= 2:
                            dve.wait_ge(out_stored, (f - 2) * 16 + 16)
                        nc.vector.tensor_tensor(res[:, pf], G("f", p, F_OUT)[:, :].rearrange("p (t c) -> p t c", t=NT),
                                                xin[:, pf], ALU.add).then_inc(dve_x1, 1)

                def ln2(n):
                    if ffn and n == 0:
                        dve.wait_ge(dve_x1, f + 1)
                        stats1(res[:, pf], st2, ln2_step)
                    elif ffn and n == 1:
                        stats2(f, st2, mv2, ln2_step)
                    elif ffn and n == 2:
                        stats3(f, mv2, ve2, ln2_step, ln2_var)
                    elif ffn:
                        dve.wait_ge(ln2_rstd, f + 1)
                        nc.vector.scalar_tensor_tensor(nb2[:], mv2[:, :, 0], -1.0, rs2[:], ALU.mult,
                                                       ALU.mult).then_inc(ln2_bias, 1)
                        for t in (2, 3):
                            last = nc.vector.tensor_scalar(x2n[:, t, :], res[:, pf, t, :], mv2[:, t, 0:1],
                                                           rs2[:, t:t + 1], ALU.subtract, ALU.mult)
                        last.then_inc(dve_x2n, 1)

                def ln1(n):
                    if nxt and n == 0:
                        dve.wait_ge(x_loaded, (b + 1) * 16 + 16)
                        stats1(xin[:, 1 - p], st1, ln1_step)
                    elif nxt and n == 1:
                        stats2(b + 1, st1, mv1, ln1_step)
                    elif nxt and n == 2:
                        stats3(b + 1, mv1, ve1, ln1_step, ln1_var)
                    elif nxt:
                        normalise(b + 1, xn, xin[:, 1 - p], mv1, rs1, ln1_rstd, xn_ready)

                def route(n):
                    if not ffn:
                        return
                    if n > 0:
                        dve.wait_ge(dve_route, f * ROUTE + n)
                    if n == 0:
                        dve.wait_ge(act_lg, f + 1)
                        ins = nc.vector.tensor_tensor(lg[:], lgc[:, :, 0:9], lgc[:, :, 9:18], ALU.add)
                    elif n == 1:
                        nc.vector.tensor_scalar(dd[:, :, 8], lg[:, :, 8], -1.0, None, ALU.mult)
                        for t in range(NT):
                            ins = nc.vector.max(mx[:, t, :], lg[:, t, 0:E])
                    elif n == 2:
                        ins = nc.vector.tensor_tensor(dd[:, :, 0:E], lg[:, :, 0:E], per(mx[:, :, 0], E),
                                                      ALU.subtract)
                    elif n == 3:
                        nc.vector.memset(carrier[:], 0.0)
                        for t in range(NT):
                            ins = nc.vector.max_index(ix[:, t, :], mx[:, t, :], lg[:, t, 0:E])
                    elif n == 4:
                        ins = nc.vector.tensor_tensor(m0[:], rep(iota, NT), per(ix[:, :, 0], E), ALU.is_equal)
                    elif n == 5:
                        ins = nc.vector.tensor_tensor(m1[:], rep(iota, NT), per(ix[:, :, 1], E), ALU.is_equal)
                    elif n == 6:
                        ins = nc.vector.tensor_tensor(m0[:], m0[:], m1[:], ALU.add)
                    elif n == 7:
                        dve.wait_ge(act_exp, f + 1)
                        ins = nc.vector.tensor_reduce(den[:, :, 0], ee[:, :, 0:E], AX.X, ALU.add)
                    elif n == 8:
                        ins = nc.vector.tensor_scalar(den[:, :, 1], ee[:, :, 8], 1.0, None, ALU.add)
                    elif n == 9:
                        ins = nc.vector.tensor_tensor(em[:], ee[:, :, 0:E], m0[:], ALU.mult)
                    elif n == 10:
                        ins = nc.vector.reciprocal(rden[:], den[:])
                    elif n == 11:
                        ins = nc.vector.tensor_tensor(cw[:, :, 0:E], em[:], per(rden[:, :, 0], E), ALU.mult)
                    else:
                        ins = nc.vector.tensor_copy(cw[:, :, 8], rden[:, :, 1])
                    ins.then_inc(dve_route, 1)

                if att:
                    dve.wait_ge(act_xhi, b + 1)
                    low(xT_lo[:], A(A_XT)[:, :], xT_hi[:], dve_xlo)
                gn_sums()
                gn_square()
                combine(0, 0)
                gn_variance()
                half(0)
                half(1)
                gn_affine()
                combine(0, 1)
                half(2)
                combine(1, 0)
                half(3)
                residual()
                ln2(0)
                if att:
                    dve.wait_ge(a_full, b * A_USES + A_QT + 1)
                    nc.vector.tensor_tensor(qt[:].rearrange("p (t i) -> p t i", t=NT),
                                            A(A_QT)[:, :].rearrange("p (t i) -> p t i", t=NT),
                                            rep(g_up, NT), ALU.mult).then_inc(dve_qt, 1)
                ln2(1)
                combine(1, 1)
                ln2(2)
                combine(2, 0)
                k_decay(0)
                ln2(3)
                combine(2, 1)
                k_decay(1)
                combine(3, 0)
                if ffn:
                    dve.wait_ge(act_x2hi, f + 1)
                    low(x2T_lo[:], G("f", p, F_XT)[:, :], x2T_hi[:], dve_x2lo)
                scores(0, 0)
                combine(3, 1)
                scores(0, 1)
                scores(0, 2)
                route(0)
                state_add(0)
                route(1)
                state_mask(0)
                route(2)
                scores(1, 0)
                route(3)
                if ffn:
                    dve.wait_ge(f_full, f * F_USES + F_UP + 1)
                    dve.wait_ge(act_silu, f * SILU + 1)
                    nc.vector.tensor_tensor(hh[:, 8, :], G("f", p, F_UP)[:, :], gate[:],
                                            ALU.mult).then_inc(dve_up, 1)
                scores(1, 1)
                route(4)
                scores(1, 2)
                route(5)
                state_add(1)
                ln1(0)
                state_mask(1)
                scores(2, 0)
                route(6)
                ln1(1)
                scores(2, 1)
                ln1(2)
                route(7)
                scores(2, 2)
                route(8)
                state_add(2)
                route(9)
                scores(3, 0)
                route(10)
                state_mask(2)
                ln1(3)
                scores(3, 1)
                route(11)
                scores(3, 2)
                route(12)
                if not later(b):
                    dve.wait_ge(wf_loaded, 16 * 5)
                    nc.vector.tensor_copy(rw_s[:, 0:9], rw[:])
                    nc.vector.tensor_copy(w1_hi[:], w1[:]).then_inc(setup_ffn_hi, 1)
                    dve.wait_ge(setup_ffn_hi, 1)
                    nc.vector.tensor_tensor(rw_s[:, 9:18], rw[:], rw_s[:, 0:9].bitcast(f32), ALU.subtract)
                    nc.vector.tensor_tensor(w1_lo[:], w1[:], w1_hi[:].bitcast(f32),
                                            ALU.subtract).then_inc(setup_ffn, 1)

            dve.wait_ge(x_loaded, 16)
            stats1(xin[:, 0], st1, ln1_step)
            stats2(0, st1, mv1, ln1_step)
            stats3(0, mv1, ve1, ln1_step, ln1_var)
            normalise(0, xn, xin[:, 0], mv1, rs1, ln1_rstd, xn_ready)
            wh = bass.AP(wqkv[:].tensor, 0, [list(wqkv[:].ap[0]), [HALF, 4], [0, 2], [1, HALF]])
            dve.wait_ge(w_loaded, 16 * 2)
            nc.vector.memset(rw_s[:].bitcast(f32), 0.0)
            nc.vector.tensor_copy(sel[:], mats[:, 5:9, :])
            nc.vector.tensor_copy(wh_hi[:], wh)
            nc.vector.tensor_copy(wqkv_hi[:], wqkv[:]).then_inc(setup_hi, 1)
            dve.wait_ge(setup_hi, 1)
            nc.vector.tensor_tensor(wh_lo[:], wh, wh_hi[:].bitcast(f32), ALU.subtract)
            nc.vector.tensor_tensor(wqkv_lo[:], wqkv[:], wqkv_hi[:].bitcast(f32), ALU.subtract).then_inc(setup_dve, 1)
            iterations(dve, steps)

        @block.tensor
        def _(pe):
            def tile(x, t):
                return x[:, t * P:t * P + P]

            def three(out, w_hi, w_lo, x_hi, x_lo):
                nc.tensor.matmul(out, w_hi, x_hi, start=True, stop=False)
                nc.tensor.matmul(out, w_hi, x_lo, start=False, stop=False)
                return nc.tensor.matmul(out, w_lo, x_hi, start=False, stop=True)

            def steps(b, p, att, ffn, moe, nxt):
                f, m = b - 1, b - 2

                def wait_a(u):
                    if u >= RA or later(b):
                        pe.wait_ge(*freed_a(b, u))

                def wait_g(what, u):
                    free = freed_g(b, what, u)
                    if free:
                        pe.wait_ge(*free)

                def half(n):
                    if att:
                        if n == 0:
                            pe.wait_ge(dve_xlo, b + 1)
                        wait_a(A_HALF + n)
                        three(A(A_HALF + n)[:, :], wh_hi[:, n].rearrange("p x c -> p (x c)"),
                              wh_lo[:, n].rearrange("p x c -> p (x c)"), xT_hi[:], xT_lo[:]).then_inc(a_full, 1)

                def q_terms(n):
                    if att:
                        wait_a(A_SELQ[n])
                        nc.tensor.matmul(A(A_SELQ[n])[:, :], sel[:, n % 2, :], halves[:, n // 2, :],
                                         start=True, stop=True).then_inc(a_full, 1)

                def k_terms(n):
                    if att:
                        if n == 0:
                            pe.wait_ge(dve_half, b * 4 + 4)
                        wait_a(A_SELK + n)
                        q = QUADS[n]
                        nc.tensor.matmul(A(A_SELK + n)[:, :], sel[:, 2 + q % 2, :], halves[:, 2 + q // 2, :],
                                         start=True, stop=True).then_inc(a_full, 1)

                def kv(n):
                    if att:
                        wait_a(A_KV + n)
                        for t in (2 * n, 2 * n + 1):
                            last = three(A(A_KV + n)[:, t % 2 * 2 * C:t % 2 * 2 * C + 2 * C], tile(xT_hi, t),
                                         tile(xT_lo, t), wqkv_hi[:, C:3 * C], wqkv_lo[:, C:3 * C])
                        last.then_inc(a_full, 1)

                def scores(t, q):
                    if att:
                        if t == 0 and q == QUADS[0]:
                            pe.wait_ge(q_spread, b * 16 * HQ + 16 * HQ)
                        wait_a(a_s(t, q))
                        nc.tensor.matmul(A(a_s(t, q))[:, :], tile(k4[:, q, :], t),
                                         qbd[:, q, t].rearrange("p h i -> p (h i)"),
                                         start=True, stop=True).then_inc(a_full, 1)

                def update(t):
                    if att:
                        pe.wait_ge(dve_kt, b * (NT // 2) + t // 2 + 1)
                        wait_a(a_u(t))
                        nc.tensor.matmul(A(a_u(t))[:, 0:C], kt[:, t, :], diag(t), start=True,
                                         stop=True).then_inc(a_full, 1)

                def values(t):
                    if not att:
                        return
                    if t == 0:
                        pe.wait_ge(act_v, b * NT + NT)
                        if later(b):
                            pe.wait_ge(act_yn, b)
                    else:
                        pe.wait_ge(dve_statem, b * (NT - 1) + t)
                        nc.tensor.matmul(tile(bankY, t), state_m[:, t - 1, :], tile(qt, t), start=True, stop=False,
                                         skip_group_check=True)
                    pe.wait_ge(dve_s, b * DQ * NT + DQ * t + DQ)
                    pe.wait_ge(pool_s, b * NT + t + 1)
                    for h in range(HQ):
                        for q in range(NQ):
                            rows = slice(32 * q, 32 * q + 32)
                            last = nc.tensor.matmul(bankY[rows, t * P:t * P + P], vbd[:, t, h, rows],
                                                    sm[:, t % 2, q, h * P:h * P + P],
                                                    start=(t == 0 and h == 0), stop=(h == HQ - 1),
                                                    skip_group_check=True)
                    last.then_inc(y_full, 1)

                def up(u):
                    if ffn:
                        n = {F_GATE: 8, F_UP: 9}.get(u, u - F_EXP)
                        wait_g("f", u)
                        three(G("f", p, u)[:, :], w1_hi[:, n * C:n * C + C], w1_lo[:, n * C:n * C + C], x2T_hi[:],
                              x2T_lo[:]).then_inc(f_full, 1)

                def down(t, g):
                    if moe:
                        if t == 0 and g == 0:
                            pe.wait_ge(act_silu, m * SILU + SILU)
                            pe.wait_ge(dve_up, m + 1)
                        wait_g("m", 3 * t + g)
                        for n, e in enumerate(GROUPS[g]):
                            last = nc.tensor.matmul(G("m", p, 3 * t + g)[:, n * C:n * C + C],
                                                    tile(hh[:, e, :], t), w2[:, e * C:e * C + C],
                                                    start=True, stop=True)
                        last.then_inc(m_full, 1)

                if att:
                    pe.wait_ge(xn_ready, b + 1)
                    wait_a(A_XT)
                    for t in range(NT):
                        last = nc.tensor.transpose(tile(A(A_XT), t), xn[:, t, :], ident)
                    last.then_inc(a_full, 1)
                down(0, 0)
                down(0, 1)
                down(0, 2)
                half(0)
                if ffn:
                    pe.wait_ge(gn_stats, f + 1)
                    wait_g("f", F_GN)
                    nc.tensor.matmul(G("f", p, F_GN)[:, 0:2], avg8, gmv[:], start=True, stop=True).then_inc(f_full, 1)
                half(1)
                down(1, 0)
                half(2)
                half(3)
                q_terms(0)
                down(1, 1)
                if ffn:
                    pe.wait_ge(act_yn, f + 1)
                    wait_g("f", F_OUT)
                    for t in range(NT):
                        last = nc.tensor.matmul(tile(G("f", p, F_OUT), t), tile(yn, t), wo[:], start=True, stop=True)
                    last.then_inc(f_full, 1)
                q_terms(1)
                down(1, 2)
                if att:
                    wait_a(A_QT)
                    three(A(A_QT)[:, :], wqkv_hi[:, 0:C], wqkv_lo[:, 0:C], xT_hi[:], xT_lo[:]).then_inc(a_full, 1)
                q_terms(2)
                q_terms(3)
                down(2, 0)
                kv(0)
                down(2, 1)
                kv(1)
                down(2, 2)
                k_terms(0)
                down(3, 0)
                k_terms(1)
                if ffn:
                    pe.wait_ge(act_x2n, f + 1)
                    pe.wait_ge(dve_x2n, f + 1)
                    wait_g("f", F_XT)
                    for t in range(NT):
                        last = nc.tensor.transpose(tile(G("f", p, F_XT), t), x2n[:, t, :], ident)
                    last.then_inc(f_full, 1)
                k_terms(2)
                k_terms(3)
                down(3, 1)
                down(3, 2)
                scores(0, 3)
                scores(0, 0)
                scores(0, 1)
                scores(0, 2)
                update(0)
                if ffn:
                    pe.wait_ge(dve_x2lo, f + 1)
                    if not later(f):
                        pe.wait_ge(setup_ffn, 1)
                    wait_g("f", F_LG)
                    for t in range(NT):
                        lgs = G("f", p, F_LG)[:, 32 * t:32 * t + 2 * C]
                        nc.tensor.matmul(lgs, tile(x2T_hi, t), rw_s[:], start=True, stop=False,
                                         skip_group_check=True)
                        last = nc.tensor.matmul(lgs, tile(x2T_lo, t), rw_s[:], start=False, stop=True,
                                                skip_group_check=True)
                    last.then_inc(f_full, 1)
                up(F_GATE)
                scores(1, 3)
                up(F_UP)
                scores(1, 0)
                up(F_EXP + 0)
                scores(1, 1)
                values(0)
                scores(1, 2)
                update(1)
                up(F_EXP + 1)
                scores(2, 3)
                up(F_EXP + 2)
                scores(2, 0)
                values(1)
                scores(2, 1)
                up(F_EXP + 3)
                scores(2, 2)
                update(2)
                scores(3, 3)
                up(F_EXP + 4)
                scores(3, 0)
                values(2)
                up(F_EXP + 5)
                scores(3, 1)
                scores(3, 2)
                up(F_EXP + 6)
                up(F_EXP + 7)
                values(3)

            pe.wait_ge(w_loaded, 16 * 2)
            pe.wait_ge(setup_dve, 1)
            pe.wait_ge(setup_pool, 3)
            iterations(pe, steps)


def constants():
    import numpy as np
    lo, hi = np.float32(np.log(1.0 - 0.999)), np.float32(np.log(1.0 - 0.9))
    gamma = (np.float32(1) - np.exp(np.linspace(lo, hi, H, dtype=np.float32))).astype(np.float64)
    i = np.arange(P)
    dist = i[None, :] - i[:, None]
    decay = np.where(dist[:, None, :] >= 0, gamma[None, :, None] ** np.maximum(dist, 0)[:, None, :], 0.0)
    gp = np.repeat(gamma, HD)
    head = np.arange(C) // HD
    mats = np.zeros((P, 10, P))
    mats[:, 0] = np.eye(P)
    mats[:, 1] = gp[:, None] ** (i[None, :] + 1)
    mats[:, 2] = gp[None, :] ** (P - 1 - i[:, None])
    mats[:, 3] = head[:, None] == head[None, :]
    mats[:, 4] = (head[:, None] == head[None, :]) / HD
    for which, parts in enumerate(((0, 1, 0, 1), (0, 0, 1, 1))):
        for n in range(2):
            for h in range(HQ):
                for term, part in enumerate(parts):
                    for a in range(HD):
                        mats[part * HALF + (HQ * n + h) * HD + a, 5 + 2 * which + n, h * 32 + term * HD + a] = 1
    mats[:, 9, 0] = gp ** P
    mats[:, 9, 8:8 + E] = np.arange(E)
    return decay.astype(np.float32), mats.astype(np.float32)


def kernel(**inputs):
    import numpy as np
    import concourse.bacc as bacc
    from concourse import mybir as mb
    from concourse.bass_utils import run_bass_kernel_spmd

    g = {k.split("_", 1)[1]: np.asarray(v) for k, v in inputs.items()}
    decay, mats = constants()

    def columns(w):
        return np.transpose(w, (1, 0, 2)).reshape(w.shape[1], -1)

    arrays = {
        "x": g["attn_x"],
        "wqkv": np.concatenate([g["attn_wq"].T, g["attn_wk"].T, g["attn_wv"].T], axis=1),
        "wo": g["attn_wo"].T,
        "w1": np.concatenate([columns(g["ffn_w1"]), g["ffn_shared_gate_up"]], axis=1),
        "w2": np.concatenate([columns(g["ffn_w2"]), g["ffn_shared_down"]], axis=1),
        "rw": np.concatenate([g["ffn_router_w"], g["ffn_shared_gate_w"]], axis=1),
        "gn": np.stack([g["attn_gn_w"], g["attn_gn_b"]], axis=1),
        "decay": decay,
        "mats": mats,
    }
    arrays = {f"in_{k}": np.ascontiguousarray(v) for k, v in arrays.items()}
    nc = bacc.Bacc("TRN2", target_bir_lowering=False, num_devices=1)
    args = [nc.dram_tensor(k, v.shape, mb.dt.from_np(v.dtype), kind="ExternalInput").ap() for k, v in arrays.items()]
    out = nc.dram_tensor("out", (B, T, C), mb.dt.float32, kind="ExternalOutput").ap()
    preln_layer_kernel(nc, *args, out)
    r = run_bass_kernel_spmd(nc, [arrays], core_ids=[0])
    return r.results[0]["out"]
```

```python
import concourse.bass as bass
from concourse import mybir
from contextlib import ExitStack

B, T, C = 16, 512, 128
H, HD = 16, 8
E = 8
P = 128
NT = T // P
HQ = 4
NQ = H // HQ
HALF = C // 2
EPS = 1e-5

RA = 3
STARTS = ("x", "q", "k", "q4")
A_ORDER = [("kv", 0), ("kv", 1), ("k4", 0), ("k4", 1), ("k4", 2), ("k4", 3), ("s", 0, 3), ("s", 0, 0),
           ("s", 0, 1), ("s", 0, 2), ("u", 0), ("s", 1, 3), ("s", 1, 0), ("s", 1, 1), ("s", 1, 2), ("u", 1),
           ("s", 2, 3), ("s", 2, 0), ("s", 2, 1), ("s", 2, 2), ("u", 2), ("s", 3, 3), ("s", 3, 0), ("x",),
           ("s", 3, 1), ("s", 3, 2), ("q",), ("k",), ("q4", 0), ("q4", 1), ("q4", 2), ("q4", 3)]
A_USES = sum(use[0] not in STARTS for use in A_ORDER)
N_USES = len(A_ORDER) - A_USES
F_GN, F_OUT, F_XT, F_LG, F_GATE, F_UP, F_EXP, F_USES = 0, 1, 2, 3, 4, 5, 6, 14
M_USES = 3 * NT
GROUPS = [(0, 1, 2, 3), (4, 5), (6, 7, 8)]
RG = 4
G_ORDER = [("m", 0), ("f", 0), ("m", 1), ("m", 2), ("m", 3), ("f", 1), ("m", 4), ("m", 5), ("m", 6), ("m", 7),
           ("m", 8), ("m", 9), ("f", 2), ("m", 10), ("m", 11), ("f", 3), ("f", 4), ("f", 5), ("f", 6), ("f", 7),
           ("f", 8), ("f", 9), ("f", 10), ("f", 11), ("f", 12), ("f", 13)]
G_USES = len(G_ORDER)
G_TAIL = [("m", 0), ("m", 1), ("f", 0), ("m", 2), ("m", 3), ("m", 4), ("m", 5), ("f", 1), ("m", 6), ("m", 7),
          ("m", 8), ("m", 9), ("f", 2), ("m", 10), ("m", 11), ("f", 3), ("f", 4), ("f", 5), ("f", 6), ("f", 7),
          ("f", 8), ("f", 9), ("f", 10), ("f", 11), ("f", 12), ("f", 13)]
LAG = {"f": 1, "m": 2}
DQ = 3
QUADS = [3, 0, 1, 2]
SILU = 9
MOE = 6
ROUTE = 13


def a_count(seq, *use):
    own = [u for u in A_ORDER if (u[0] in STARTS) == (use[0] in STARTS)]
    return seq * len(own) + own.index(use) + 1


def a_before(*use):
    at = A_ORDER.index(use) - RA
    return A_ORDER[at] if at >= 0 else None


def g_order(b):
    return G_TAIL if isinstance(b, int) and b >= B else G_ORDER


def later(b):
    return not isinstance(b, int) or b > 0


def preln_layer_kernel(nc, x_d, wqkv_d, wo_d, w1_d, w2_d, rw_d, gn_d, decay_d, mats_d, out_d):
    f32 = mybir.dt.float32
    f32r = mybir.dt.float32r
    ALU = mybir.AluOpType
    ACT = mybir.ActivationFunctionType
    AX = mybir.AxisListType

    x_v = x_d.rearrange("b (t p) c -> b p t c", p=P)
    out_v = out_d.rearrange("b (t p) c -> b p t c", p=P)

    ctx = ExitStack()
    with ctx:
        def sb(name, shape, dt=f32):
            return ctx.enter_context(nc.sbuf_tensor(name, shape, dt))

        def sem(name):
            return ctx.enter_context(nc.semaphore(name))

        decay = sb("decay", [P, H, P])
        mats = sb("mats", [P, 10, P])
        ident, g_up, g_down, bdmask, avg8 = (mats[:, n, :] for n in range(5))
        gC, iota = mats[:, 9, 0:1], mats[:, 9, 8:8 + E]
        sel = sb("sel", [P, 4, P], f32r)
        gnp = sb("gnp", [P, 2])
        wqkv = sb("wqkv", [P, 3 * C])
        wo = sb("wo", [P, C])
        w1 = sb("w1", [P, 10 * C])
        w2 = sb("w2", [P, 9 * C])
        rw = sb("rw", [P, 9])
        wqkv_hi = sb("wqkv_hi", [P, 3 * C], f32r)
        wqkv_lo = sb("wqkv_lo", [P, 3 * C], f32r)
        w1_hi = sb("w1_hi", [P, 10 * C], f32r)
        w1_lo = sb("w1_lo", [P, 10 * C], f32r)
        xin = sb("xin", [P, 2, NT, C])
        xn = sb("xn", [P, NT, C])
        xT_hi = sb("xT_hi", [P, T], f32r)
        xT_lo = sb("xT_lo", [P, T], f32r)
        halves = sb("halves", [P, 4, T], f32r)
        qt = sb("qt", [P, 2, NT - 1, P])
        q4 = sb("q4", [P, NQ, T], f32r)
        k4 = sb("k4", [P, NQ, T], f32r)
        qbd = sb("qbd", [P, NQ, NT, HQ, P], f32r)
        kt = sb("kt", [P, NT, C])
        vbd = sb("vbd", [P, NT, HQ, C])
        sm = sb("sm", [P, 2, NQ, HQ * P])
        s_raw = sb("s_raw", [P, 2, HQ * P])
        state = sb("state", [P, C])
        state_m = sb("state_m", [P, NT - 1, C])
        yn = sb("yn", [P, T])
        st1 = sb("st1", [P, NT, 6])
        mv1 = sb("mv1", [P, NT, 2])
        ve1 = sb("ve1", [P, NT])
        rs1 = sb("rs1", [P, NT])
        gst = sb("gst", [P, 6])
        gmv = sb("gmv", [P, 2])
        gm = sb("gm", [P, 2])
        gvar = sb("gvar", [P, 1])
        gve = sb("gve", [P, 1])
        grs = sb("grs", [P, 1])
        gab = sb("gab", [P, 2])
        mhalf = sb("mhalf", [P, NT])
        res = sb("res", [P, 2, NT, C])
        st2 = sb("st2", [P, NT, 6])
        mv2 = sb("mv2", [P, NT, 2])
        ve2 = sb("ve2", [P, NT])
        rs2 = sb("rs2", [P, NT])
        x2n = sb("x2n", [P, NT, C])
        x2T = sb("x2T", [P, T])
        x2T_hi = sb("x2T_hi", [P, T], f32r)
        x2T_lo = sb("x2T_lo", [P, T], f32r)
        lg = sb("lg", [P, NT, 9])
        mx = sb("mx", [P, NT, 8])
        ix = sb("ix", [P, NT, 8], mybir.dt.uint32)
        dd = sb("dd", [P, NT, 9])
        ee = sb("ee", [P, NT, 9])
        m0 = sb("m0", [P, NT, 8])
        m1 = sb("m1", [P, NT, 8])
        den = sb("den", [P, NT, 2])
        rden = sb("rden", [P, NT, 2])
        em = sb("em", [P, NT, 8])
        cw = sb("cw", [P, 2, NT, 9])
        gate = sb("gate", [P, T])
        hh = sb("hh", [P, 2, 9, T])
        carrier = sb("carrier", [P, 1])
        nb2 = sb("nb2", [P, NT])
        accs = sb("accs", [P, 2, 4, C])
        warm = sb("warm", [P, 1])

        bankA = [ctx.enter_context(nc.psum_tensor(f"bankA{i}", [P, 512], f32)) for i in range(RA)]
        bankY = ctx.enter_context(nc.psum_tensor("bankY", [P, T], f32))
        bankG = [ctx.enter_context(nc.psum_tensor(f"bankG{i}", [P, 512], f32)) for i in range(RG)]

        def A(*use):
            return bankA[A_ORDER.index(use) % RA]

        def bank_g(order, p, what, u):
            return bankG[(p * G_USES + order.index((what, u))) % RG]

        def diag(t):
            v = vbd[:, t, 0, :]
            return bass.AP(v.tensor, v.offset, [list(v.ap[0]), [HQ * HD, NQ], [C + HD, HQ], [1, HD]])

        def per(v, n):
            return bass.AP(v.tensor, v.offset, [list(p) for p in v.ap] + [[0, n]])

        def rep(v, n):
            return bass.AP(v.tensor, v.offset, [list(v.ap[0]), [0, n]] + [list(p) for p in v.ap[1:]])

        w_loaded = sem("w_loaded")
        x_loaded = sem("x_loaded")
        q_spread = sem("q_spread")
        out_stored = sem("out_stored")
        setup_pool = sem("setup_pool")
        setup_hi = sem("setup_hi")
        setup_dve = sem("setup_dve")
        ln1_rstd = sem("ln1_rstd")
        ln1_centred = sem("ln1_centred")
        xn_ready = sem("xn_ready")
        ln2_rstd = sem("ln2_rstd")
        gn_rstd = sem("gn_rstd")
        pool_s = sem("pool_s")
        a_full = sem("a_full")
        n_full = sem("n_full")
        f_full = sem("f_full")
        m_full = sem("m_full")
        y_full = sem("y_full")
        act_xhi = sem("act_xhi")
        act_half = sem("act_half")
        act_q4 = sem("act_q4")
        act_k4 = sem("act_k4")
        act_v = sem("act_v")
        act_s = sem("act_s")
        act_yn = sem("act_yn")
        act_x2n = sem("act_x2n")
        act_x2hi = sem("act_x2hi")
        act_lg = sem("act_lg")
        act_exp = sem("act_exp")
        act_silu = sem("act_silu")
        ln1_step = sem("ln1_step")
        ln1_var = sem("ln1_var")
        dve_xlo = sem("dve_xlo")
        dve_half = sem("dve_half")
        dve_qt = sem("dve_qt")
        dve_kt = sem("dve_kt")
        dve_s = sem("dve_s")
        dve_state = sem("dve_state")
        dve_statem = sem("dve_statem")
        gn_step = sem("gn_step")
        gn_stats = sem("gn_stats")
        gn_mean = sem("gn_mean")
        gn_diff = sem("gn_diff")
        gn_var = sem("gn_var")
        gn_scale = sem("gn_scale")
        gn_ab = sem("gn_ab")
        dve_x1 = sem("dve_x1")
        ln2_step = sem("ln2_step")
        ln2_var = sem("ln2_var")
        dve_x2n = sem("dve_x2n")
        dve_x2lo = sem("dve_x2lo")
        dve_route = sem("dve_route")
        dve_up = sem("dve_up")
        dve_moe = sem("dve_moe")
        pool_moe = sem("pool_moe")
        pool_out = sem("pool_out")
        act_moe = sem("act_moe")
        act_warm = sem("act_warm")
        ln2_bias = sem("ln2_bias")
        decay_loaded = sem("decay_loaded")
        wf_loaded = sem("wf_loaded")
        setup_ffn_hi = sem("setup_ffn_hi")
        setup_ffn = sem("setup_ffn")

        A_FREED = {("x",): (dve_xlo, 1, 1), ("q",): (dve_qt, 1, 1), ("k",): (dve_half, 4, 4)}
        for n in range(NQ):
            A_FREED["q4", n] = act_q4, NQ, n + 1
            A_FREED["k4", n] = act_k4, NQ, n + 1
        for n in range(NT // 2):
            A_FREED["kv", n] = dve_kt, NT // 2, n + 1
        for t in range(NT):
            A_FREED["s", t, DQ] = act_s, NT, t + 1
            A_FREED["u", t] = dve_state, NT - 1, t + 1
            for q in range(DQ):
                A_FREED["s", t, q] = dve_s, DQ * NT, DQ * t + q + 1
        F_FREED = [(gn_mean, 1, 1), (dve_x1, 1, 1), (dve_x2lo, 1, 1), (act_lg, 1, 1), (act_silu, SILU, 1),
                   (dve_up, 1, 1)] + [(act_silu, SILU, 2 + e) for e in range(E)]
        M_FREED = [(dve_moe, MOE * NT, MOE * t + g) for t in range(NT) for g in (4, 6, 0)]
        M_FREED[2::3] = [(act_moe, 3 * NT, 3 * t + 3) for t in range(NT)]
        def freed_a(b, *use):
            at = A_ORDER.index(use)
            bank = at % RA
            while True:
                at -= RA
                if at < 0:
                    at, b = max(u for u in range(len(A_ORDER)) if u % RA == bank), b - 1
                was = A_ORDER[at]
                seq = b + 1 if was[0] in STARTS else b
                if not isinstance(b, int) or 0 <= seq < B:
                    s, per_seq, k = A_FREED[was]
                    return s, seq * per_seq + k
                if b < -1:
                    return None

        def freed_g(b, what, u):
            at = g_order(b).index((what, u)) - RG
            while True:
                if at < 0:
                    at, b = at + G_USES, b - 1
                was, v = g_order(b)[at]
                if not isinstance(b, int) or 0 <= b - LAG[was] < B:
                    s, per_seq, k = (F_FREED if was == "f" else M_FREED)[v]
                    return s, (b - LAG[was]) * per_seq + k
                if b < 0:
                    return None
                at -= RG

        def sequence(dram, b):
            return dram[b] if isinstance(b, int) else dram[bass.ds(b, 1)].rearrange("o p t c -> (o p) t c")

        block = ctx.enter_context(nc.Block())

        def iterations(eng, steps):
            steps(-1, 1, False, False, False, True)
            steps(0, 0, True, False, False, True)
            steps(1, 1, True, True, False, True)
            steps(2, 0, True, True, True, True)
            with eng.Fori(0, (B - 4) // 4) as k:
                for i in range(4):
                    steps(4 * k + 3 + i, (i + 1) % 2, True, True, True, True)
            steps(B - 1, 1, True, True, True, False)
            steps(B, 0, False, True, True, False)
            steps(B + 1, 1, False, False, True, False)

        @block.sync
        def _(sp):
            def steps(b, p, att, ffn, moe, nxt):
                if att:
                    sp.wait_ge(act_q4, b * NQ + NQ)
                    if later(b):
                        sp.wait_ge(a_full, (b - 1) * A_USES + A_USES)
                    else:
                        sp.wait_ge(setup_pool, 3)
                    for h in range(HQ):
                        rows = slice(32 * h, 32 * h + 32)
                        sp.dma_start(qbd[rows, :, :, h, :].bitcast(f32),
                                     q4[rows, :, :].rearrange("p q (t i) -> p q t i", t=NT).bitcast(f32)
                                     ).then_inc(q_spread, 16)
                if nxt:
                    if not isinstance(b, int) or b > 0:
                        sp.wait_ge(dve_x1, b)
                    elif att:
                        sp.wait_ge(ln1_step, 1)
                    sp.dma_start(xin[:, 1 - p], sequence(x_v, b + 1)).then_inc(x_loaded, 16)
                if nxt and not att:
                    sp.dma_start(wqkv[:], wqkv_d).then_inc(w_loaded, 16)
                    sp.dma_start(mats[:], mats_d).then_inc(w_loaded, 16)
                    sp.dma_start(decay[:], decay_d).then_inc(decay_loaded, 16)
                    for dst, src in ((gnp[:], gn_d), (wo[:], wo_d), (rw[:], rw_d), (w1[:], w1_d), (w2[:], w2_d)):
                        sp.dma_start(dst, src).then_inc(wf_loaded, 16)
                if moe:
                    sp.wait_ge(pool_out, (b - 2) * NT + NT)
                    sp.dma_start(sequence(out_v, b - 2), res[:, p]).then_inc(out_stored, 16)

            iterations(sp, steps)
            sp.wait_ge(out_stored, 16 * B)

        @block.gpsimd
        def _(pool):
            nc.gpsimd.memset(mhalf[:], -0.5).then_inc(setup_pool, 1)

            def steps(b, p, att, ffn, moe, nxt):
                f, m = b - 1, b - 2

                def total(t):
                    if moe:
                        acc = accs[:, t % 2]
                        pool.wait_ge(act_moe, m * 3 * NT + 3 * t + 3)
                        pool.wait_ge(dve_moe, m * MOE * NT + MOE * t + MOE)
                        nc.gpsimd.tensor_tensor(acc[:, 0:2, :], acc[:, 0:2, :], acc[:, 2:4, :],
                                                ALU.add).then_inc(pool_moe, 1)
                        pool.wait_ge(pool_moe, m * 2 * NT + 2 * t + 1)
                        nc.gpsimd.tensor_tensor(acc[:, 0, :], acc[:, 0, :], acc[:, 1, :],
                                                ALU.add).then_inc(pool_moe, 1)
                        pool.wait_ge(pool_moe, m * 2 * NT + 2 * t + 2)
                        nc.gpsimd.tensor_tensor(res[:, p, t, :], res[:, p, t, :], acc[:, 0, :],
                                                ALU.add).then_inc(pool_out, 1)

                def scores(t):
                    if att:
                        pool.wait_ge(act_s, b * NT + t + 1)
                        nc.gpsimd.tensor_tensor(sm[:, t % 2, DQ, :], s_raw[:, t % 2, :],
                                                decay[:, HQ * DQ:, :].rearrange("p h i -> p (h i)"),
                                                ALU.mult).then_inc(pool_s, 1)

                def zeros():
                    if nxt and not att:
                        nc.gpsimd.memset(vbd[:], 0.0).then_inc(setup_pool, 1)
                        nc.gpsimd.memset(qbd[:].bitcast(f32), 0.0).then_inc(setup_pool, 1)
                        pool.wait_ge(decay_loaded, 16)

                def rstd_gn():
                    if ffn:
                        pool.wait_ge(gn_var, f + 1)
                        nc.gpsimd.tensor_tensor(grs[:], gve[:], mhalf[:, 0:1], ALU.pow).then_inc(gn_rstd, 1)

                def rstd_ln2():
                    if ffn:
                        pool.wait_ge(ln2_var, f + 1)
                        nc.gpsimd.tensor_tensor(rs2[:], ve2[:], mhalf[:], ALU.pow).then_inc(ln2_rstd, 1)

                def rstd_ln1():
                    if nxt:
                        if not att:
                            pool.wait_ge(setup_pool, 1)
                        pool.wait_ge(ln1_var, b + 2)
                        nc.gpsimd.tensor_tensor(rs1[:], ve1[:], mhalf[:], ALU.pow).then_inc(ln1_rstd, 1)

                def normalise():
                    if nxt:
                        nc.gpsimd.tensor_tensor(xn[:], xin[:, 1 - p], per(mv1[:, :, 0], C),
                                                ALU.subtract).then_inc(ln1_centred, 1)
                        pool.wait_ge(ln1_rstd, b + 2)
                        pool.wait_ge(ln1_centred, b + 2)
                        nc.gpsimd.tensor_tensor(xn[:], xn[:], per(rs1[:], C), ALU.mult).then_inc(xn_ready, 1)

                if not (att or nxt):
                    rstd_gn()
                    total(0)
                    total(1)
                    rstd_ln2()
                    total(2)
                    total(3)
                    return
                rstd_gn()
                total(0)
                rstd_ln2()
                scores(0)
                total(1)
                total(2)
                scores(1)
                rstd_ln1()
                normalise()
                zeros()
                scores(2)
                scores(3)
                total(3)

            iterations(pool, steps)

        @block.scalar
        def _(act):
            def copy(out, in_):
                return nc.scalar.activation(out, in_, ACT.Copy)

            def steps(b, p, att, ffn, moe, nxt):
                n1, f, m = b + 1, b - 1, b - 2

                def G(what, p, u):
                    return bank_g(g_order(b), p, what, u)

                def high(n):
                    if nxt:
                        act.wait_ge(n_full, a_count(n1, "qk"[n // 2]))
                        rows = slice(n % 2 * HALF, n % 2 * HALF + HALF)
                        copy(halves[rows, n, :], A("qk"[n // 2])[rows, :]).then_inc(act_half, 1)

                def q_terms(n):
                    if nxt:
                        act.wait_ge(n_full, a_count(n1, "q4", n))
                        if n == 0 and att:
                            act.wait_ge(q_spread, b * 16 * HQ + 16 * HQ)
                        copy(q4[:, n, :], A("q4", n)[:, :]).then_inc(act_q4, 1)

                def k_terms(n):
                    if att:
                        act.wait_ge(a_full, a_count(b, "k4", n))
                        copy(k4[:, QUADS[n], :], A("k4", n)[:, :]).then_inc(act_k4, 1)

                def values(n):
                    if att:
                        if n == 0 and not later(b):
                            act.wait_ge(setup_pool, 2)
                        act.wait_ge(a_full, a_count(b, "kv", n))
                        for t in (0, 1):
                            v = A("kv", n)[:, t * 2 * C + C:t * 2 * C + 2 * C]
                            copy(diag(2 * n + t), v.rearrange("p (q h c) -> p q h c", q=NQ, h=HQ)).then_inc(act_v, 1)

                def weigh(t):
                    if moe:
                        act.wait_ge(m_full, m * M_USES + 3 * t + 3)
                        if t == 0:
                            act.wait_ge(dve_route, m * ROUTE + ROUTE)
                        if t >= 2 or later(m):
                            act.wait_ge(pool_out, m * NT + t - 1)
                        for n, e in enumerate(GROUPS[2]):
                            nc.scalar.activation(accs[:, t % 2, n, :], G("m", p, 3 * t + 2)[:, n * C:n * C + C], ACT.Copy,
                                                 scale=cw[:, p, t, e:e + 1]).then_inc(act_moe, 1)

                def scores(t):
                    if att:
                        act.wait_ge(a_full, a_count(b, "s", t, DQ))
                        if t >= 2 or later(b):
                            act.wait_ge(pool_s, b * NT + t - 1)
                        copy(s_raw[:, t % 2, :], A("s", t, DQ)[:, :]).then_inc(act_s, 1)

                def silu(e):
                    if ffn:
                        act.wait_ge(f_full, f * F_USES + F_EXP + e + 1)
                        nc.scalar.activation(hh[:, 1 - p, e, :], G("f", p, F_EXP + e)[:, :], ACT.Silu).then_inc(act_silu, 1)

                def x_high():
                    if nxt:
                        act.wait_ge(n_full, a_count(n1, "x"))
                        copy(xT_hi[:], A("x")[:, :]).then_inc(act_xhi, 1)

                def group_norm():
                    if ffn:
                        act.wait_ge(gn_ab, f + 1)
                        nc.scalar.activation(yn[:], bankY[:, :], ACT.Identity, scale=gab[:, 0:1],
                                             bias=gab[:, 1:2]).then_inc(act_yn, 1)

                def layer_norm():
                    if ffn:
                        act.wait_ge(ln2_bias, f + 1)
                        for t in (0, 1):
                            last = nc.scalar.activation(x2n[:, t, :], res[:, 1 - p, t, :], ACT.Identity,
                                                        scale=rs2[:, t:t + 1], bias=nb2[:, t:t + 1])
                        last.then_inc(act_x2n, 1)

                def x2_high():
                    if ffn:
                        act.wait_ge(f_full, f * F_USES + F_XT + 1)
                        copy(x2T_hi[:], G("f", p, F_XT)[:, :])
                        copy(x2T[:], G("f", p, F_XT)[:, :]).then_inc(act_x2hi, 1)

                def exp_table():
                    if ffn:
                        nc.scalar.activation(warm[:], gnp[:, 0:1], ACT.Exp).then_inc(act_warm, 1)

                def logits():
                    if ffn:
                        act.wait_ge(f_full, f * F_USES + F_LG + 1)
                        if later(f):
                            act.wait_ge(dve_route, (f - 1) * ROUTE + 4)
                        copy(lg[:], G("f", p, F_LG)[:, 0:16 * NT].rearrange("p (t c) -> p t c", t=NT)[:, :, 0:9]
                             ).then_inc(act_lg, 1)

                def exponents():
                    if ffn:
                        act.wait_ge(dve_route, f * ROUTE + 3)
                        nc.scalar.activation(ee[:], dd[:], ACT.Exp).then_inc(act_exp, 1)

                def silu_gate():
                    if ffn:
                        act.wait_ge(f_full, f * F_USES + F_GATE + 1)
                        if later(f):
                            act.wait_ge(dve_up, f)
                        nc.scalar.activation(gate[:], G("f", p, F_GATE)[:, :], ACT.Silu).then_inc(act_silu, 1)

                if not (att or nxt):
                    weigh(0)
                    group_norm()
                    weigh(1)
                    layer_norm()
                    weigh(2)
                    x2_high()
                    weigh(3)
                    logits()
                    silu_gate()
                    exp_table()
                    exponents()
                    silu(0)
                    silu(1)
                    silu(2)
                    silu(3)
                    silu(4)
                    silu(5)
                    silu(6)
                    silu(7)
                    return
                weigh(0)
                values(0)
                group_norm()
                values(1)
                k_terms(0)
                k_terms(1)
                k_terms(2)
                weigh(1)
                k_terms(3)
                scores(0)
                layer_norm()
                x2_high()
                scores(1)
                weigh(2)
                exp_table()
                logits()
                weigh(3)
                scores(2)
                exponents()
                silu_gate()
                silu(0)
                silu(1)
                silu(2)
                x_high()
                scores(3)
                silu(3)
                high(0)
                high(1)
                high(2)
                silu(4)
                silu(5)
                high(3)
                q_terms(0)
                silu(6)
                silu(7)
                q_terms(1)
                q_terms(2)
                q_terms(3)

            act.wait_ge(setup_pool, 1)
            nc.scalar.activation(warm[:], mhalf[:, 0:1], ACT.Copy).then_inc(act_warm, 1)
            iterations(act, steps)

        @block.vector
        def _(dve):
            def low(dst, full, hi, ready):
                nc.vector.tensor_tensor(dst, full, hi.bitcast(f32), ALU.subtract).then_inc(ready, 1)

            def stats1(src, st, step):
                for t in range(NT):
                    last = nc.vector.bn_stats(st[:, t, :], src[:, t, :])
                last.then_inc(step, 1)

            def stats2(b, st, mv, step):
                dve.wait_ge(step, 2 * b + 1)
                nc.vector.memset(carrier[:], 0.0)
                for t in range(NT):
                    last = nc.vector.bn_aggr(mv[:, t, :], st[:, t, :])
                last.then_inc(step, 1)

            def stats3(b, mv, ve, step, var):
                dve.wait_ge(step, 2 * b + 2)
                nc.vector.tensor_scalar(ve[:], mv[:, :, 1], EPS, None, ALU.add).then_inc(var, 1)

            def steps(b, p, att, ffn, moe, nxt):
                n1, f, m, pf, pn = b + 1, b - 1, b - 2, 1 - p, 1 - p

                def G(what, p, u):
                    return bank_g(g_order(b), p, what, u)

                def low_half(n):
                    if nxt:
                        if n % 2 == 0:
                            dve.wait_ge(act_half, n1 * 4 + n + 2)
                        rows, other = slice(0, HALF), slice(HALF, C)
                        if n % 2:
                            rows, other = other, rows
                        low(halves[other, n, :], A("qk"[n // 2])[rows, :], halves[rows, n, :], dve_half)

                def q_decay():
                    if nxt:
                        nc.vector.tensor_tensor(qt[:, pn], A("q")[:, P:].rearrange("p (t i) -> p t i", i=P),
                                                rep(g_up, NT - 1), ALU.mult).then_inc(dve_qt, 1)

                def k_decay(n):
                    if att:
                        dve.wait_ge(act_v, b * NT + 2 * n + 2)
                        nc.vector.tensor_tensor(kt[:, 2 * n:2 * n + 2, :],
                                                A("kv", n)[:, :].rearrange("p (t c) -> p t c", t=2)[:, :, 0:C],
                                                rep(g_down, 2), ALU.mult).then_inc(dve_kt, 1)

                def scores(t, q):
                    if att:
                        if not later(b) and t == 0 and q == 0:
                            dve.wait_ge(decay_loaded, 16)
                        dve.wait_ge(a_full, a_count(b, "s", t, q))
                        nc.vector.tensor_tensor(sm[:, t % 2, q, :].rearrange("p (h i) -> p h i", h=HQ),
                                                A("s", t, q)[:, :].rearrange("p (h i) -> p h i", h=HQ),
                                                decay[:, HQ * q:HQ * q + HQ, :], ALU.mult).then_inc(dve_s, 1)

                def state_add(t):
                    if att:
                        dve.wait_ge(a_full, a_count(b, "u", t))
                        if t == 0:
                            nc.vector.tensor_copy(state[:], A("u", t)[:, 0:C]).then_inc(dve_state, 1)
                        else:
                            nc.vector.scalar_tensor_tensor(state[:], state[:], gC, A("u", t)[:, 0:C],
                                                           ALU.mult, ALU.add).then_inc(dve_state, 1)

                def state_mask(t):
                    if att:
                        dve.wait_ge(dve_state, b * (NT - 1) + t + 1)
                        nc.vector.tensor_tensor(state_m[:, t, :], state[:], bdmask, ALU.mult).then_inc(dve_statem, 1)

                def combine(t, g):
                    if not moe:
                        return
                    dve.wait_ge(m_full, m * M_USES + 3 * t + g + 1)
                    for n, e in enumerate(GROUPS[g]):
                        y, w = G("m", p, 3 * t + g)[:, n * C:n * C + C], cw[:, p, t, e:e + 1]
                        acc = accs[:, t % 2, 3, :] if e % 2 else res[:, p, t, :]
                        if e >= 2:
                            dve.wait_ge(dve_moe, m * MOE * NT + MOE * t + e - 1)
                        if e == 1:
                            if t >= 2 or later(m):
                                dve.wait_ge(pool_out, m * NT + t - 1)
                            nc.vector.tensor_scalar(acc, y, w, None, ALU.mult).then_inc(dve_moe, 1)
                        else:
                            nc.vector.scalar_tensor_tensor(acc, y, w, acc, ALU.mult, ALU.add).then_inc(dve_moe, 1)

                def gn_sums():
                    if ffn:
                        dve.wait_ge(y_full, f * NT + NT)
                        nc.vector.bn_stats(gst[:], bankY[:, :]).then_inc(gn_step, 1)
                        dve.wait_ge(gn_step, 2 * f + 1)
                        nc.vector.memset(carrier[:], 0.0)
                        nc.vector.bn_aggr(gmv[:], gst[:]).then_inc(gn_step, 1)

                def gn_square():
                    if ffn:
                        dve.wait_ge(gn_step, 2 * f + 2)
                        nc.vector.scalar_tensor_tensor(gmv[:, 1:2], gmv[:, 0:1], gmv[:, 0:1], gmv[:, 1:2],
                                                       ALU.mult, ALU.add).then_inc(gn_stats, 1)

                def gn_variance():
                    if ffn:
                        dve.wait_ge(f_full, f * F_USES + F_GN + 1)
                        nc.vector.tensor_copy(gm[:], G("f", p, F_GN)[:, 0:2]).then_inc(gn_mean, 1)
                        dve.wait_ge(gn_mean, f + 1)
                        nc.vector.scalar_tensor_tensor(gvar[:], gm[:, 0:1], gm[:, 0:1], gm[:, 1:2], ALU.mult,
                                                       ALU.subtract, reverse1=True).then_inc(gn_diff, 1)
                        dve.wait_ge(gn_diff, f + 1)
                        nc.vector.tensor_scalar(gve[:], gvar[:], 0.0, EPS, ALU.max, ALU.add).then_inc(gn_var, 1)

                def gn_affine():
                    if ffn:
                        dve.wait_ge(gn_rstd, f + 1)
                        nc.vector.tensor_tensor(gab[:, 0:1], grs[:], gnp[:, 0:1], ALU.mult).then_inc(gn_scale, 1)
                        dve.wait_ge(gn_scale, f + 1)
                        nc.vector.scalar_tensor_tensor(gab[:, 1:2], gm[:, 0:1], gab[:, 0:1], gnp[:, 1:2], ALU.mult,
                                                       ALU.subtract, reverse1=True).then_inc(gn_ab, 1)

                def residual():
                    if ffn:
                        dve.wait_ge(f_full, f * F_USES + F_OUT + 1)
                        if not isinstance(b, int) or f >= 2:
                            dve.wait_ge(out_stored, (f - 2) * 16 + 16)
                        nc.vector.tensor_tensor(res[:, pf], G("f", p, F_OUT)[:, :].rearrange("p (t c) -> p t c", t=NT),
                                                xin[:, pf], ALU.add).then_inc(dve_x1, 1)

                def ln2(n):
                    if ffn and n == 0:
                        dve.wait_ge(dve_x1, f + 1)
                        stats1(res[:, pf], st2, ln2_step)
                    elif ffn and n == 1:
                        stats2(f, st2, mv2, ln2_step)
                    elif ffn and n == 2:
                        stats3(f, mv2, ve2, ln2_step, ln2_var)
                    elif ffn:
                        dve.wait_ge(ln2_rstd, f + 1)
                        nc.vector.scalar_tensor_tensor(nb2[:], mv2[:, :, 0], -1.0, rs2[:], ALU.mult,
                                                       ALU.mult).then_inc(ln2_bias, 1)
                        for t in (2, 3):
                            last = nc.vector.tensor_scalar(x2n[:, t, :], res[:, pf, t, :], mv2[:, t, 0:1],
                                                           rs2[:, t:t + 1], ALU.subtract, ALU.mult)
                        last.then_inc(dve_x2n, 1)

                def ln1(n):
                    if nxt and n == 0:
                        dve.wait_ge(x_loaded, (b + 1) * 16 + 16)
                        stats1(xin[:, 1 - p], st1, ln1_step)
                    elif nxt and n == 1:
                        stats2(b + 1, st1, mv1, ln1_step)
                    elif nxt and n == 2:
                        stats3(b + 1, mv1, ve1, ln1_step, ln1_var)

                def route(n):
                    if not ffn:
                        return
                    if n > 1:
                        dve.wait_ge(dve_route, f * ROUTE + n)
                    if n == 0:
                        dve.wait_ge(act_lg, f + 1)
                        ins = nc.vector.tensor_scalar(dd[:, :, 8], lg[:, :, 8], -1.0, None, ALU.mult)
                    elif n == 1:
                        for t in range(NT):
                            ins = nc.vector.max(mx[:, t, :], lg[:, t, 0:E])
                    elif n == 2:
                        ins = nc.vector.tensor_tensor(dd[:, :, 0:E], lg[:, :, 0:E], per(mx[:, :, 0], E),
                                                      ALU.subtract)
                    elif n == 3:
                        nc.vector.memset(carrier[:], 0.0)
                        for t in range(NT):
                            ins = nc.vector.max_index(ix[:, t, :], mx[:, t, :], lg[:, t, 0:E])
                    elif n == 4:
                        ins = nc.vector.tensor_tensor(m0[:], rep(iota, NT), per(ix[:, :, 0], E), ALU.is_equal)
                    elif n == 5:
                        ins = nc.vector.tensor_tensor(m1[:], rep(iota, NT), per(ix[:, :, 1], E), ALU.is_equal)
                    elif n == 6:
                        ins = nc.vector.tensor_tensor(m0[:], m0[:], m1[:], ALU.add)
                    elif n == 7:
                        dve.wait_ge(act_exp, f + 1)
                        ins = nc.vector.tensor_reduce(den[:, :, 0], ee[:, :, 0:E], AX.X, ALU.add)
                    elif n == 8:
                        ins = nc.vector.tensor_scalar(den[:, :, 1], ee[:, :, 8], 1.0, None, ALU.add)
                    elif n == 9:
                        ins = nc.vector.tensor_tensor(em[:], ee[:, :, 0:E], m0[:], ALU.mult)
                    elif n == 10:
                        ins = nc.vector.reciprocal(rden[:], den[:])
                    elif n == 11:
                        ins = nc.vector.tensor_tensor(cw[:, pf, :, 0:E], em[:], per(rden[:, :, 0], E), ALU.mult)
                    else:
                        ins = nc.vector.tensor_copy(cw[:, pf, :, 8], rden[:, :, 1])
                    ins.then_inc(dve_route, 1)

                def x_low():
                    if nxt:
                        dve.wait_ge(act_xhi, n1 + 1)
                        low(xT_lo[:], A("x")[:, :], xT_hi[:], dve_xlo)

                def x2_low():
                    if ffn:
                        dve.wait_ge(act_x2hi, f + 1)
                        low(x2T_lo[:], G("f", p, F_XT)[:, :], x2T_hi[:], dve_x2lo)

                def shared_up():
                    if ffn:
                        dve.wait_ge(f_full, f * F_USES + F_UP + 1)
                        dve.wait_ge(act_silu, f * SILU + 1)
                        nc.vector.tensor_tensor(hh[:, pf, 8, :], G("f", p, F_UP)[:, :], gate[:],
                                                ALU.mult).then_inc(dve_up, 1)

                def split_projections():
                    if nxt and not att:
                        dve.wait_ge(w_loaded, 16 * 2)
                        nc.vector.tensor_copy(sel[:], mats[:, 5:9, :])
                        nc.vector.tensor_copy(wqkv_hi[:], wqkv[:]).then_inc(setup_hi, 1)
                        dve.wait_ge(setup_hi, 1)
                        nc.vector.tensor_tensor(wqkv_lo[:], wqkv[:], wqkv_hi[:].bitcast(f32),
                                                ALU.subtract).then_inc(setup_dve, 1)

                def split_weights():
                    if att and not later(b):
                        dve.wait_ge(wf_loaded, 16 * 5)
                        nc.vector.tensor_copy(w1_hi[:], w1[:]).then_inc(setup_ffn_hi, 1)
                        dve.wait_ge(setup_ffn_hi, 1)
                        nc.vector.tensor_tensor(w1_lo[:], w1[:], w1_hi[:].bitcast(f32),
                                                ALU.subtract).then_inc(setup_ffn, 1)

                if not (att or nxt):
                    gn_sums()
                    gn_square()
                    combine(0, 0)
                    gn_variance()
                    combine(0, 1)
                    gn_affine()
                    combine(1, 0)
                    combine(1, 1)
                    residual()
                    ln2(0)
                    ln2(1)
                    ln2(2)
                    combine(2, 0)
                    ln2(3)
                    combine(2, 1)
                    combine(3, 0)
                    x2_low()
                    combine(3, 1)
                    route(0)
                    route(1)
                    route(2)
                    shared_up()
                    route(3)
                    route(4)
                    route(5)
                    route(6)
                    route(7)
                    route(8)
                    route(9)
                    route(10)
                    route(11)
                    route(12)
                    return
                gn_sums()
                gn_square()
                combine(0, 0)
                gn_variance()
                combine(0, 1)
                gn_affine()
                combine(1, 0)
                k_decay(0)
                k_decay(1)
                residual()
                combine(1, 1)
                ln2(0)
                split_weights()
                ln2(1)
                ln2(2)
                combine(2, 0)
                scores(0, 0)
                ln2(3)
                scores(0, 1)
                scores(0, 2)
                state_add(0)
                combine(2, 1)
                combine(3, 0)
                ln1(0)
                x2_low()
                scores(1, 0)
                combine(3, 1)
                scores(1, 1)
                ln1(1)
                state_mask(0)
                ln1(2)
                scores(1, 2)
                split_projections()
                state_add(1)
                route(0)
                route(1)
                route(2)
                route(3)
                state_mask(1)
                scores(2, 0)
                scores(2, 1)
                scores(2, 2)
                route(4)
                state_add(2)
                route(5)
                route(6)
                route(7)
                state_mask(2)
                scores(3, 0)
                shared_up()
                route(8)
                x_low()
                scores(3, 1)
                scores(3, 2)
                low_half(0)
                low_half(1)
                route(9)
                q_decay()
                route(10)
                route(11)
                low_half(2)
                low_half(3)
                route(12)

            iterations(dve, steps)

        @block.tensor
        def _(pe):
            def tile(x, t):
                return x[:, t * P:t * P + P]

            def three(out, w_hi, w_lo, x_hi, x_lo):
                nc.tensor.matmul(out, w_hi, x_hi, start=True, stop=False)
                nc.tensor.matmul(out, w_hi, x_lo, start=False, stop=False)
                return nc.tensor.matmul(out, w_lo, x_hi, start=False, stop=True)

            def steps(b, p, att, ffn, moe, nxt):
                n1, f, m = b + 1, b - 1, b - 2

                def G(what, p, u):
                    return bank_g(g_order(b), p, what, u)

                def wait_a(*use):
                    free = freed_a(b, *use)
                    if free:
                        pe.wait_ge(*free)

                def wait_g(what, u):
                    free = freed_g(b, what, u)
                    if free:
                        pe.wait_ge(*free)

                def project(what):
                    if nxt:
                        if what == "q":
                            if not att:
                                pe.wait_ge(setup_dve, 1)
                            pe.wait_ge(dve_xlo, n1 + 1)
                        wait_a(what)
                        cols = slice(0, C) if what == "q" else slice(C, 2 * C)
                        three(A(what)[:, :], wqkv_hi[:, cols], wqkv_lo[:, cols], xT_hi[:], xT_lo[:]).then_inc(n_full, 1)

                def q_terms(n):
                    if nxt:
                        if n % 2 == 0 and a_before("q4", n) != ("k",):
                            pe.wait_ge(dve_half, n1 * 4 + n // 2 + 1)
                        wait_a("q4", n)
                        nc.tensor.matmul(A("q4", n)[:, :], sel[:, n % 2, :], halves[:, n // 2, :],
                                         start=True, stop=True).then_inc(n_full, 1)

                def k_terms(n):
                    if att:
                        if n == 0:
                            pe.wait_ge(dve_half, b * 4 + 4)
                        wait_a("k4", n)
                        q = QUADS[n]
                        nc.tensor.matmul(A("k4", n)[:, :], sel[:, 2 + q % 2, :], halves[:, 2 + q // 2, :],
                                         start=True, stop=True).then_inc(a_full, 1)

                def kv(n):
                    if att:
                        wait_a("kv", n)
                        for t in (2 * n, 2 * n + 1):
                            last = three(A("kv", n)[:, t % 2 * 2 * C:t % 2 * 2 * C + 2 * C], tile(xT_hi, t),
                                         tile(xT_lo, t), wqkv_hi[:, C:3 * C], wqkv_lo[:, C:3 * C])
                        last.then_inc(a_full, 1)

                def scores(t, q):
                    if att:
                        if t == 0 and q == QUADS[0]:
                            pe.wait_ge(q_spread, b * 16 * HQ + 16 * HQ)
                        before = a_before("s", t, q)
                        if t == 0 and before and before[0] == "k4":
                            pe.wait_ge(act_k4, b * NQ + max(before[1], QUADS.index(q)) + 1)
                        else:
                            if t == 0:
                                pe.wait_ge(act_k4, b * NQ + QUADS.index(q) + 1)
                            wait_a("s", t, q)
                        nc.tensor.matmul(A("s", t, q)[:, :], tile(k4[:, q, :], t),
                                         qbd[:, q, t].rearrange("p h i -> p (h i)"),
                                         start=True, stop=True).then_inc(a_full, 1)

                def update(t):
                    if att:
                        pe.wait_ge(dve_kt, b * (NT // 2) + t // 2 + 1)
                        wait_a("u", t)
                        nc.tensor.matmul(A("u", t)[:, 0:C], kt[:, t, :], diag(t), start=True,
                                         stop=True).then_inc(a_full, 1)

                def values(t):
                    if not att:
                        return
                    if t == 0:
                        pe.wait_ge(act_v, b * NT + NT)
                        if later(b):
                            pe.wait_ge(act_yn, b)
                    else:
                        pe.wait_ge(dve_statem, b * (NT - 1) + t)
                        nc.tensor.matmul(tile(bankY, t), state_m[:, t - 1, :], qt[:, p, t - 1, :], start=True, stop=False,
                                         skip_group_check=True)
                    pe.wait_ge(dve_s, b * DQ * NT + DQ * t + DQ)
                    pe.wait_ge(pool_s, b * NT + t + 1)
                    for h in range(HQ):
                        for q in range(NQ):
                            rows = slice(32 * q, 32 * q + 32)
                            last = nc.tensor.matmul(bankY[rows, t * P:t * P + P], vbd[:, t, h, rows],
                                                    sm[:, t % 2, q, h * P:h * P + P],
                                                    start=(t == 0 and h == 0), stop=(h == HQ - 1),
                                                    skip_group_check=True)
                    last.then_inc(y_full, 1)

                def up(u):
                    if ffn:
                        n = {F_GATE: 8, F_UP: 9}.get(u, u - F_EXP)
                        if u == F_GATE:
                            pe.wait_ge(dve_x2lo, f + 1)
                        wait_g("f", u)
                        three(G("f", p, u)[:, :], w1_hi[:, n * C:n * C + C], w1_lo[:, n * C:n * C + C], x2T_hi[:],
                              x2T_lo[:]).then_inc(f_full, 1)

                def down(t, g):
                    if moe:
                        if t == 0 and g == 0:
                            pe.wait_ge(act_silu, m * SILU + SILU)
                            pe.wait_ge(dve_up, m + 1)
                        wait_g("m", 3 * t + g)
                        for n, e in enumerate(GROUPS[g]):
                            last = nc.tensor.matmul(G("m", p, 3 * t + g)[:, n * C:n * C + C],
                                                    tile(hh[:, p, e, :], t), w2[:, e * C:e * C + C],
                                                    start=True, stop=True)
                        last.then_inc(m_full, 1)

                def transpose_x():
                    if nxt:
                        if not att:
                            pe.wait_ge(w_loaded, 16 * 2)
                        pe.wait_ge(xn_ready, n1 + 1)
                        wait_a("x")
                        for t in range(NT):
                            last = nc.tensor.transpose(tile(A("x"), t), xn[:, t, :], ident)
                        last.then_inc(n_full, 1)

                def head_means():
                    if ffn:
                        pe.wait_ge(gn_stats, f + 1)
                        wait_g("f", F_GN)
                        nc.tensor.matmul(G("f", p, F_GN)[:, 0:2], avg8, gmv[:], start=True, stop=True).then_inc(f_full, 1)

                def output():
                    if ffn:
                        pe.wait_ge(act_yn, f + 1)
                        wait_g("f", F_OUT)
                        for t in range(NT):
                            last = nc.tensor.matmul(tile(G("f", p, F_OUT), t), tile(yn, t), wo[:], start=True, stop=True)
                        last.then_inc(f_full, 1)

                def transpose_x2():
                    if ffn:
                        pe.wait_ge(act_x2n, f + 1)
                        pe.wait_ge(dve_x2n, f + 1)
                        wait_g("f", F_XT)
                        for t in range(NT):
                            last = nc.tensor.transpose(tile(G("f", p, F_XT), t), x2n[:, t, :], ident)
                        last.then_inc(f_full, 1)

                def logits():
                    if ffn:
                        pe.wait_ge(act_x2hi, f + 1)
                        if not later(f):
                            pe.wait_ge(setup_ffn, 1)
                        wait_g("f", F_LG)
                        for t in range(NT):
                            last = nc.tensor.matmul(G("f", p, F_LG)[:, 16 * t:16 * t + 9], tile(x2T, t), rw[:],
                                                    start=True, stop=True)
                        last.then_inc(f_full, 1)

                if not (att or nxt):
                    down(0, 0)
                    down(0, 1)
                    head_means()
                    down(0, 2)
                    down(1, 0)
                    down(1, 1)
                    down(1, 2)
                    output()
                    down(2, 0)
                    down(2, 1)
                    down(2, 2)
                    down(3, 0)
                    transpose_x2()
                    down(3, 1)
                    down(3, 2)
                    logits()
                    up(F_GATE)
                    up(F_UP)
                    up(F_EXP + 0)
                    up(F_EXP + 1)
                    up(F_EXP + 2)
                    up(F_EXP + 3)
                    up(F_EXP + 4)
                    up(F_EXP + 5)
                    up(F_EXP + 6)
                    up(F_EXP + 7)
                    return
                down(0, 0)
                head_means()
                down(0, 1)
                down(0, 2)
                kv(0)
                down(1, 0)
                kv(1)
                k_terms(0)
                output()
                down(1, 1)
                k_terms(1)
                k_terms(2)
                down(1, 2)
                down(2, 0)
                k_terms(3)
                scores(0, 3)
                down(2, 1)
                scores(0, 0)
                down(2, 2)
                scores(0, 1)
                scores(0, 2)
                down(3, 0)
                update(0)
                transpose_x2()
                scores(1, 3)
                scores(1, 0)
                scores(1, 1)
                values(0)
                down(3, 1)
                scores(1, 2)
                down(3, 2)
                logits()
                up(F_GATE)
                up(F_UP)
                update(1)
                scores(2, 3)
                up(F_EXP + 0)
                up(F_EXP + 1)
                scores(2, 0)
                scores(2, 1)
                scores(2, 2)
                values(1)
                update(2)
                up(F_EXP + 2)
                scores(3, 3)
                scores(3, 0)
                transpose_x()
                values(2)
                scores(3, 1)
                scores(3, 2)
                up(F_EXP + 3)
                project("q")
                project("k")
                up(F_EXP + 4)
                up(F_EXP + 5)
                up(F_EXP + 6)
                up(F_EXP + 7)
                q_terms(0)
                values(3)
                q_terms(1)
                q_terms(2)
                q_terms(3)

            iterations(pe, steps)


def constants():
    import numpy as np
    lo, hi = np.float32(np.log(1.0 - 0.999)), np.float32(np.log(1.0 - 0.9))
    gamma = (np.float32(1) - np.exp(np.linspace(lo, hi, H, dtype=np.float32))).astype(np.float64)
    i = np.arange(P)
    dist = i[None, :] - i[:, None]
    decay = np.where(dist[:, None, :] >= 0, gamma[None, :, None] ** np.maximum(dist, 0)[:, None, :], 0.0)
    gp = np.repeat(gamma, HD)
    head = np.arange(C) // HD
    mats = np.zeros((P, 10, P))
    mats[:, 0] = np.eye(P)
    mats[:, 1] = gp[:, None] ** (i[None, :] + 1)
    mats[:, 2] = gp[None, :] ** (P - 1 - i[:, None])
    mats[:, 3] = head[:, None] == head[None, :]
    mats[:, 4] = (head[:, None] == head[None, :]) / HD
    for which, parts in enumerate(((0, 1, 0, 1), (0, 0, 1, 1))):
        for n in range(2):
            for h in range(HQ):
                for term, part in enumerate(parts):
                    for a in range(HD):
                        mats[part * HALF + (HQ * n + h) * HD + a, 5 + 2 * which + n, h * 32 + term * HD + a] = 1
    mats[:, 9, 0] = gp ** P
    mats[:, 9, 8:8 + E] = np.arange(E)
    return decay.astype(np.float32), mats.astype(np.float32)


def kernel(**inputs):
    import numpy as np
    import concourse.bacc as bacc
    from concourse import mybir as mb
    from concourse.bass_utils import run_bass_kernel_spmd

    g = {k.split("_", 1)[1]: np.asarray(v) for k, v in inputs.items()}
    decay, mats = constants()

    def columns(w):
        return np.transpose(w, (1, 0, 2)).reshape(w.shape[1], -1)

    arrays = {
        "x": g["attn_x"],
        "wqkv": np.concatenate([g["attn_wq"].T, g["attn_wk"].T, g["attn_wv"].T], axis=1),
        "wo": g["attn_wo"].T,
        "w1": np.concatenate([columns(g["ffn_w1"]), g["ffn_shared_gate_up"]], axis=1),
        "w2": np.concatenate([columns(g["ffn_w2"]), g["ffn_shared_down"]], axis=1),
        "rw": np.concatenate([g["ffn_router_w"], g["ffn_shared_gate_w"]], axis=1),
        "gn": np.stack([g["attn_gn_w"], g["attn_gn_b"]], axis=1),
        "decay": decay,
        "mats": mats,
    }
    arrays = {f"in_{k}": np.ascontiguousarray(v) for k, v in arrays.items()}
    nc = bacc.Bacc("TRN2", target_bir_lowering=False, num_devices=1)
    args = [nc.dram_tensor(k, v.shape, mb.dt.from_np(v.dtype), kind="ExternalInput").ap() for k, v in arrays.items()]
    out = nc.dram_tensor("out", (B, T, C), mb.dt.float32, kind="ExternalOutput").ap()
    preln_layer_kernel(nc, *args, out)
    r = run_bass_kernel_spmd(nc, [arrays], core_ids=[0])
    return r.results[0]["out"]
```
